# Optimizing a Trainium2 kernel written in Bass

```python
import numpy as np
import jax
import jax.numpy as jnp

def _softmax(x, axis=-1):
    return jax.nn.softmax(x, axis=axis)

def _gelu(x):
    return jax.nn.gelu(x, approximate=True)

def _silu(x):
    return jax.nn.silu(x)

def _sigmoid(x):
    return jax.nn.sigmoid(x)

def _layernorm(x, axis=-1, eps=1e-05):
    m = jnp.mean(x, axis=axis, keepdims=True)
    v = jnp.var(x, axis=axis, keepdims=True)
    return (x - m) / jnp.sqrt(v + eps)

def _scatter_add(tgt, idx, src, axis=0):
    return tgt.at[idx].add(src)

def _segment_sum(src, seg, n):
    return jax.ops.segment_sum(src, seg, n)
kernel_name = 'mk_adaln_d2_jaxref_r8_2eeb36'

def setup_inputs(seed: int=0):
    np.random.seed(seed)
    _w = jnp.asarray

    def _L0_attn_setup():
        import jax, jax.numpy as jnp
        import numpy as np
        HEADS = 8
        DIM_HEAD = 64
        SCALE = DIM_HEAD ** (-0.5)
        key = jax.random.key(seed)
        ks = jax.random.split(key, 6)
        b, n, d = (2, 512, 128)
        inner = HEADS * DIM_HEAD
        x = jax.random.normal(ks[0], (b, n, d), dtype=jnp.float32)
        Wq = jax.random.normal(ks[1], (d, inner), dtype=jnp.float32) * d ** (-0.5)
        Wk = jax.random.normal(ks[2], (d, inner), dtype=jnp.float32) * d ** (-0.5)
        Wv = jax.random.normal(ks[3], (d, inner), dtype=jnp.float32) * d ** (-0.5)
        Wout = jax.random.normal(ks[4], (inner, d), dtype=jnp.float32) * inner ** (-0.5)
        bout = jnp.zeros((d,), dtype=jnp.float32)
        return {'x': x, 'Wq': Wq, 'Wk': Wk, 'Wv': Wv, 'Wout': Wout, 'bout': bout}
    _L0_attn_in = _L0_attn_setup()

    def _L0_ffn_setup():
        import jax, jax.numpy as jnp
        import numpy as np
        EXPERT_NUM = 8
        CAPACITY = 100
        key = jax.random.key(seed)
        k1, k2, k3 = jax.random.split(key, 3)
        B, S, H, E = (8, 256, 128, EXPERT_NUM)
        x = jax.random.normal(k1, (B, S, H), dtype=jnp.float32)
        w_gate = jax.random.normal(k2, (H, E), dtype=jnp.float32) * 0.02
        w_expert = jax.random.normal(k3, (H, H), dtype=jnp.float32) * 0.02
        b_expert = jnp.zeros((H,), dtype=jnp.float32)
        return {'x': x, 'w_gate': w_gate, 'w_expert': w_expert, 'b_expert': b_expert}
    _L0_ffn_in = _L0_ffn_setup()
    _L0_c = _w((lambda *s: np.random.randn(*s).astype(np.float32) * 0.05)(16, 128))
    _L0_wmod = _w((lambda *s: np.random.randn(*s).astype(np.float32) * 0.05)(128, 6 * 128) * 128 ** (-0.5))

    def _L1_attn_setup():
        import jax, jax.numpy as jnp
        import numpy as np
        LN_EPS = 1e-05
        key = jax.random.key(seed)
        ks = jax.random.split(key, 5)
        B, S, E, H = (4, 128, 128, 16)
        sd = E ** (-0.5)
        return {'x': jax.random.normal(ks[0], (B, S, E), jnp.float32), 'Wq': jax.random.normal(ks[1], (E, E), jnp.float32) * sd, 'Wk': jax.random.normal(ks[2], (E, E), jnp.float32) * sd, 'Wv': jax.random.normal(ks[3], (E, E), jnp.float32) * sd, 'bias_table': jax.random.normal(ks[4], (2 * S - 1, H), jnp.float32) * 0.02, 'ln_gamma': jnp.ones((E,), jnp.float32), 'ln_beta': jnp.zeros((E,), jnp.float32)}
    _L1_attn_in = _L1_attn_setup()

    def _L1_ffn_setup():
        import jax, jax.numpy as jnp
        import numpy as np
        B, S, H = (2, 128, 128)
        E, F = (8, 512)
        GATE_TEMP = 0.1
        key = jax.random.key(seed)
        ks = jax.random.split(key, 6)
        s_h = 1.0 / np.sqrt(H)
        s_f = 1.0 / np.sqrt(F)
        return {'hidden_states': jax.random.normal(ks[0], (B, S, H), dtype=jnp.float32), 'w_router': jax.random.normal(ks[1], (H, E), dtype=jnp.float32) * s_h, 'w_gating': jax.random.normal(ks[2], (H, E), dtype=jnp.float32) * s_h, 'w_gate': jax.random.normal(ks[3], (E, H, F), dtype=jnp.float32) * s_h, 'w_up': jax.random.normal(ks[4], (E, H, F), dtype=jnp.float32) * s_h, 'w_down': jax.random.normal(ks[5], (E, F, H), dtype=jnp.float32) * s_f}
    _L1_ffn_in = _L1_ffn_setup()
    _L1_c = _w((lambda *s: np.random.randn(*s).astype(np.float32) * 0.05)(16, 128))
    _L1_wmod = _w((lambda *s: np.random.randn(*s).astype(np.float32) * 0.05)(128, 6 * 128) * 128 ** (-0.5))
    _d = {'L0_attn_x': _L0_attn_in['x'], 'L0_attn_Wq': _L0_attn_in['Wq'], 'L0_attn_Wk': _L0_attn_in['Wk'], 'L0_attn_Wv': _L0_attn_in['Wv'], 'L0_attn_Wout': _L0_attn_in['Wout'], 'L0_attn_bout': _L0_attn_in['bout'], 'L0_ffn_w_gate': _L0_ffn_in['w_gate'], 'L0_ffn_w_expert': _L0_ffn_in['w_expert'], 'L0_ffn_b_expert': _L0_ffn_in['b_expert'], 'L0_c': _L0_c, 'L0_wmod': _L0_wmod, 'L1_attn_Wq': _L1_attn_in['Wq'], 'L1_attn_Wk': _L1_attn_in['Wk'], 'L1_attn_Wv': _L1_attn_in['Wv'], 'L1_attn_bias_table': _L1_attn_in['bias_table'], 'L1_attn_ln_gamma': _L1_attn_in['ln_gamma'], 'L1_attn_ln_beta': _L1_attn_in['ln_beta'], 'L1_ffn_w_router': _L1_ffn_in['w_router'], 'L1_ffn_w_gating': _L1_ffn_in['w_gating'], 'L1_ffn_w_gate': _L1_ffn_in['w_gate'], 'L1_ffn_w_up': _L1_ffn_in['w_up'], 'L1_ffn_w_down': _L1_ffn_in['w_down'], 'L1_c': _L1_c, 'L1_wmod': _L1_wmod}
    _x0 = _d['L0_attn_x']
    _d['L0_attn_x'] = jax.random.normal(jax.random.fold_in(jax.random.key(seed), 1), (16, 512, 128), dtype=_x0.dtype)
    del _x0
    return _d

def reference(L0_attn_x, L0_attn_Wq, L0_attn_Wk, L0_attn_Wv, L0_attn_Wout, L0_attn_bout, L0_ffn_w_gate, L0_ffn_w_expert, L0_ffn_b_expert, L0_c, L0_wmod, L1_attn_Wq, L1_attn_Wk, L1_attn_Wv, L1_attn_bias_table, L1_attn_ln_gamma, L1_attn_ln_beta, L1_ffn_w_router, L1_ffn_w_gating, L1_ffn_w_gate, L1_ffn_w_up, L1_ffn_w_down, L1_c, L1_wmod):

    def _L0_attn_ref(x, Wq, Wk, Wv, Wout, bout):
        import jax, jax.numpy as jnp
        import numpy as np
        HEADS = 8
        DIM_HEAD = 64
        SCALE = DIM_HEAD ** (-0.5)
        b, n, _ = x.shape
        h, dh = (HEADS, DIM_HEAD)
        q = (x @ Wq).reshape(b, n, h, dh).transpose(0, 2, 1, 3)
        k = (x @ Wk).reshape(b, n, h, dh).transpose(0, 2, 1, 3)
        v = (x @ Wv).reshape(b, n, h, dh).transpose(0, 2, 1, 3)
        sim = jnp.einsum('bhid,bhjd->bhij', q, k) * SCALE
        attn = jax.nn.softmax(sim, axis=-1)
        out = jnp.einsum('bhij,bhjd->bhid', attn, v)
        out = out.transpose(0, 2, 1, 3).reshape(b, n, h * dh)
        return out @ Wout + bout

    def _L0_ffn_ref(x, w_gate, w_expert, b_expert):
        import jax, jax.numpy as jnp
        import numpy as np
        EXPERT_NUM = 8
        CAPACITY = 100
        B, S, H = x.shape
        E, C = (EXPERT_NUM, CAPACITY)
        hs = x.reshape(-1, H)
        logits = hs @ w_gate
        probs = jax.nn.softmax(logits, axis=1)
        best = jnp.argmax(probs, axis=1)
        mask = jax.nn.one_hot(best, E, dtype=jnp.int32)
        gate = jnp.sum(probs * mask.astype(probs.dtype), axis=1)
        locations = jnp.cumsum(mask, axis=0) - 1
        mask = mask * (locations < C).astype(jnp.int32)
        loc_sum = jnp.sum(locations * mask, axis=1)
        new_gates = gate[:, None] * mask.astype(probs.dtype)
        loc_oh = jax.nn.one_hot(loc_sum, C, dtype=probs.dtype)
        combine = new_gates[:, :, None] * loc_oh[:, None, :]
        dispatch = (combine != 0).astype(hs.dtype)
        dispatched = jnp.einsum('tec,th->ech', dispatch, hs).reshape(E * C, H)
        expert_out = dispatched @ w_expert + b_expert
        combined = combine.reshape(-1, E * C) @ expert_out
        return combined.reshape(B, S, H)

    def _L1_attn_ref(x, Wq, Wk, Wv, bias_table, ln_gamma, ln_beta):
        import jax, jax.numpy as jnp
        import numpy as np
        LN_EPS = 1e-05
        B, S, E = x.shape
        H = bias_table.shape[1]
        d = E // H
        scale = E ** (-0.5)
        q = (x @ Wq.T).reshape(B, S, H, d).transpose(0, 2, 1, 3)
        k = (x @ Wk.T).reshape(B, S, H, d).transpose(0, 2, 1, 3)
        v = (x @ Wv.T).reshape(B, S, H, d).transpose(0, 2, 1, 3)
        attn = jax.nn.softmax(jnp.einsum('bhsd,bhtd->bhst', q, k) * scale, axis=-1)
        rel_idx = jnp.arange(S)[:, None] - jnp.arange(S)[None, :] + (S - 1)
        rel_bias = bias_table[rel_idx].transpose(2, 0, 1)
        attn = attn + rel_bias[None]
        out = jnp.einsum('bhst,bhtd->bhsd', attn, v)
        out = out.transpose(0, 2, 1, 3).reshape(B, S, E)
        mu = out.mean(-1, keepdims=True)
        var = out.var(-1, keepdims=True)
        out = (out - mu) * jax.lax.rsqrt(var + LN_EPS) * ln_gamma + ln_beta
        return out

    def _L1_ffn_ref(hidden_states, w_router, w_gating, w_gate, w_up, w_down):
        import jax, jax.numpy as jnp
        import numpy as np
        B, S, H = (2, 128, 128)
        E, F = (8, 512)
        GATE_TEMP = 0.1
        x = hidden_states
        router_probs = jax.nn.softmax(jnp.einsum('bsh,he->bse', x, w_router), axis=-1)
        gate_weights = jax.nn.softmax(jnp.einsum('bsh,he->bse', x, w_gating) / GATE_TEMP, axis=-1)
        g = jnp.einsum('bsh,ehf->ebsf', x, w_gate)
        u = jnp.einsum('bsh,ehf->ebsf', x, w_up)
        h = jax.nn.silu(g) * u
        expert_out = jnp.einsum('ebsf,efh->ebsh', h, w_down)
        cw = router_probs * gate_weights
        cw = cw / (jnp.sum(cw, axis=-1, keepdims=True) + 1e-09)
        out = jnp.einsum('ebsh,bse->bsh', expert_out, cw)
        return out
    x = L0_attn_x
    mod = (_silu(L0_c) @ L0_wmod).reshape(L0_c.shape[0], 6, 1, -1)
    sa, ca, ga, sb, cb, gb = (mod[:, 0], mod[:, 1], mod[:, 2], mod[:, 3], mod[:, 4], mod[:, 5])
    ga = (2 * (ga >= 0) - 1) * jnp.maximum(jnp.abs(ga), 0.25)
    gb = (2 * (gb >= 0) - 1) * jnp.maximum(jnp.abs(gb), 0.25)
    h = _layernorm(x, axis=-1) * (1 + ca) + sa
    x = x + ga * _L0_attn_ref(h, L0_attn_Wq, L0_attn_Wk, L0_attn_Wv, L0_attn_Wout, L0_attn_bout)
    h = _layernorm(x, axis=-1) * (1 + cb) + sb
    x = x + gb * _L0_ffn_ref(h, L0_ffn_w_gate, L0_ffn_w_expert, L0_ffn_b_expert)
    mod = (_silu(L1_c) @ L1_wmod).reshape(L1_c.shape[0], 6, 1, -1)
    sa, ca, ga, sb, cb, gb = (mod[:, 0], mod[:, 1], mod[:, 2], mod[:, 3], mod[:, 4], mod[:, 5])
    ga = (2 * (ga >= 0) - 1) * jnp.maximum(jnp.abs(ga), 0.25)
    gb = (2 * (gb >= 0) - 1) * jnp.maximum(jnp.abs(gb), 0.25)
    h = _layernorm(x, axis=-1) * (1 + ca) + sa
    x = x + ga * _L1_attn_ref(h, L1_attn_Wq, L1_attn_Wk, L1_attn_Wv, L1_attn_bias_table, L1_attn_ln_gamma, L1_attn_ln_beta)
    h = _layernorm(x, axis=-1) * (1 + cb) + sb
    x = x + gb * _L1_ffn_ref(h, L1_ffn_w_router, L1_ffn_w_gating, L1_ffn_w_gate, L1_ffn_w_up, L1_ffn_w_down)
    return x

_drawn_inputs = setup_inputs


def setup_inputs(seed=0):
    import zlib

    import numpy as np

    out = dict(_drawn_inputs(seed))
    spreads = {'L0_attn_bout': (0.0, 0.1),
     'L0_ffn_b_expert': (0.0, 0.8),
     'L1_attn_ln_gamma': (1.0, 0.2),
     'L1_attn_ln_beta': (0.0, 0.31)}
    factors = {'L0_ffn_w_gate': 8.0, 'L0_ffn_w_expert': 8.0, 'L1_attn_Wq': 3.89, 'L1_attn_Wk': 3.946}
    for name, (base, spread) in spreads.items():
        noise = np.random.default_rng([zlib.crc32(name.encode()), seed]).standard_normal(out[name].shape)
        drawn = base * np.exp(spread * noise) if base else spread * noise
        out[name] = jnp.asarray(drawn.astype(out[name].dtype))
    for name, factor in factors.items():
        out[name] = (out[name] * factor).astype(out[name].dtype)
    return out
```

```python
import numpy as np
import concourse.bass as bass
from concourse import mybir
from concourse.alu_op_type import AluOpType as ALU
from contextlib import ExitStack

F32 = mybir.dt.float32
F32R = mybir.dt.float32r
I32 = mybir.dt.int32
ACT = mybir.ActivationFunctionType
X = mybir.AxisListType.X

B, S, D = 16, 512, 128
P = 128
NC = S // P
EPS = 1e-5
H0, DH0 = 8, 64
PAIRS = H0 // 2
E0, CAP = 8, 100
SCALE0 = DH0 ** -0.5
H1 = 16
DH1 = D // H1
G, HG = 4, 4
QR = HG * DH1
SCALE1 = D ** -0.5
TAB = 255
E1, FF = 8, 512
FC = FF // P
TEMP = 0.1
NU = 3
NF = E1 * FC


def attention0_steps():
    steps = [("v0", 0), ("proj0", 0), ("v0", 1), ("proj0", 1)]
    steps += [("max0", 0, k) for k in range(4)] + [("mt0", 0)]
    for p in range(PAIRS):
        for jc in range(NC):
            steps.append(("sc0", p, jc))
            if p + 1 < PAIRS:
                steps.append(("max0", p + 1, jc))
            if jc:
                steps.append(("pv0", p, jc - 1))
        if p + 2 < PAIRS:
            steps.append(("proj0", p + 2))
        steps.append(("pv0", p, NC - 1))
        if p + 1 < PAIRS:
            steps.append(("mt0", p + 1))
        steps.append(("z0", p))
    return steps


def attention1_steps():
    steps = [("proj1", 0), ("v1",), ("tv",), ("proj1", 1)]
    steps += [("max1", 0, k) for k in range(8)] + [("mt1", 0)]
    for g in range(G):
        for jc in range(NC):
            steps += [("sc1", g, jc, 0), ("sc1", g, jc, 1)]
            if g + 1 < G:
                steps += [("max1", g + 1, 2 * jc), ("max1", g + 1, 2 * jc + 1)]
            if jc:
                steps.append(("pv1", g, jc - 1))
            if jc == 1 and g:
                steps.append(("nat", g - 1))
        if g + 2 < G:
            steps.append(("proj1", g + 2))
        steps.append(("pv1", g, NC - 1))
        if g + 1 < G:
            steps.append(("mt1", g + 1))
        steps.append(("d1", g))
    return steps + [("nat", G - 1)]


A_STEPS = ([("load",), ("gates",), ("ln", 0), ("ht", 0)] + attention0_steps()
           + [("out0",), ("ln", 1), ("ht", 1), ("gate0",), ("pos",), ("ln", 2), ("ht", 2)]
           + attention1_steps() + [("post1",), ("ln", 4), ("ht", 3), ("route",)])


def mixture_steps():
    steps = []
    for n in range(NF + 2):
        if n < NF:
            steps.append(("gu", n))
        if n >= 2:
            steps.append(("down", n - 2))
    return steps


F_STEPS = mixture_steps()
LOOP_STEPS = F_STEPS + A_STEPS
UNITS = {"gates": 1, "ht": 1, "v0": 1, "proj0": 1, "max0": 1, "mt0": 1, "sc0": 1, "z0": 1, "out0": 1,
         "gate0": 1, "pos": 1, "v1": 1, "tv": 1, "proj1": 1, "max1": 1, "mt1": 1, "sc1": 1, "d1": 1,
         "nat": 1, "route": 1, "gu": 1}


class Phase:

    def __init__(self, steps, a, f):
        self.steps, self.a, self.f = steps, a, f
        using = [s for s in steps if s[0] in UNITS]
        first = -len(using) % NU
        self.slot, self.before, last = {}, {}, [None] * NU
        for n, s in enumerate(using):
            u = (first + n) % NU
            self.slot[s], self.before[s], last[u] = u, last[u], s
        self.last = last


class Signal:

    def __init__(self, sem, per):
        self.sem, self.per = sem, per

    def wait(self, eng, batch, n=0):
        assert -self.per <= n < self.per
        if isinstance(batch, int) and batch * self.per + n + 1 <= 0:
            return
        eng.wait_ge(self.sem, batch * self.per + (n + 1))


class Chain:

    def __init__(self, sem, per):
        self.sem, self.per, self.n = sem, per, 0

    def start(self):
        self.n = 0

    def link(self, ins):
        self.n += 1
        ins.then_inc(self.sem, 1)

    def wait(self, eng, batch):
        eng.wait_ge(self.sem, batch * self.per + self.n)

    def end(self):
        assert self.n == self.per, (self.sem, self.n)


def build_program(nc, x, cT, wmod, wqkv0, wout0, bout0, wg0, we0, be0, wqk1, wv1T, table, t_last,
                  gamma, beta, wr1, wgu1, wd1, out):
    ctx = ExitStack()
    with ctx:
        def sb(name, shape, dt=F32):
            return ctx.enter_context(nc.sbuf_tensor(name, shape, dt))

        def sem(name):
            return ctx.enter_context(nc.semaphore(name))

        def signal(name, per):
            return Signal(sem(name), per)

        w0 = sb("w0", [P, 2, 3 * H0 * DH0], F32R)
        wo = sb("wo", [P, PAIRS, D])
        bo = sb("bo", [P, D])
        wg = sb("wg", [P, E0])
        we = sb("we", [P, D])
        be = sb("be", [1, D])
        w1 = sb("w1", [P, 2, 2, G, 3, QR], F32R)
        wv = sb("wv", [P, D])
        biasd = sb("biasd", [P, H1, 2 * P])
        tlast = sb("tlast", [P, H1])
        t254 = sb("t254", [P, H1, DH1])
        wr = sb("wr", [P, 2, E1])
        wgu = sb("wgu", [P, E1, 2, FF])
        wd = sb("wd", [P, E1, FC, D])
        wgate = sb("wgate", [P, 2, 2, D])
        ident = sb("ident", [P, P])
        upper = sb("upper", [P, P])
        ones = sb("ones", [P, P])
        rev = sb("rev", [P, E0])
        mask = sb("mask", [96, HG])
        neghalf = sb("neghalf", [P, NC])
        sT = sb("sT", [P, 2, B])
        modc = sb("modc", [P, 8, B])
        gam = sb("gam", [P, D])
        bet = sb("bet", [P, D])
        xin = sb("xin", [P, NC, D])
        scb = sb("scb", [P, 2, P])
        modb = sb("modb", [P, 8])
        gates = sb("gates", [P, 4, D])
        st = sb("st", [P, NC, 6])
        mv = sb("mv", [P, NC, 2])
        ve = sb("ve", [P, NC])
        idle = sb("idle", [1, 2])
        rstd = sb("rstd", [P, NC])
        nrm = sb("nrm", [P, NC, D])
        h32 = sb("h32", [P, S])
        hT = sb("hT", [P, 2, S], F32R)
        gbo = sb("gbo", [P, D])
        xres = sb("xres", [P, NC, D])
        qk = sb("qk", [P, 2, 4, 2, S], F32R)
        V = sb("V", [P, NC, H0 * DH0])
        Pt = sb("Pt", [P, NC, 2, S])
        PS = sb("PS", [P, 2, S])
        oT = sb("oT", [P, PAIRS, S])
        rz0 = sb("rz0", [P, S])
        nm0 = sb("nm0", [P, 2, NC, 2])
        nm1 = sb("nm1", [P, 2, NC, HG])
        sm = sb("sm", [P, NC, 2, E1])
        sm2 = sb("sm2", [P, NC, 2, E1])
        sm3 = sb("sm3", [P, NC, E1])
        sc4 = sb("sc4", [P, 8, NC])
        cs = sb("cs", [P, NC, E0])
        oh = sb("oh", [P, NC, E0])
        tv = sb("tv", [P, D])
        ks = sb("ks", [96, S], F32R)
        rz1 = sb("rz1", [P, NC, HG])
        g1 = sb("g1", [P, D])
        fT = sb("fT", [P, 2, S], F32R)
        xf = sb("xf", [P, NC, D])
        gbf = sb("gbf", [P, D])
        cw = sb("cw", [P, NC, E1])
        hs = sb("hs", [P, 4, S])
        acc = sb("acc", [P, NC, D])
        ws = sb("ws", [P, 2, 2, 2, FF // 2], F32R)

        V1 = V[:, :, :].rearrange("p c (h m) -> p c h m", h=H1)
        X1 = [qk[:, i, 0, 0, :] for i in range(2)]
        K1 = [qk[:, i, 2:4, :, :].rearrange("p a b n -> p (a b) n") for i in range(2)]
        OT = [oT[:, 0:2, :].rearrange("p a n -> p (a n)")[:, 0:S + 2 * P],
              oT[:, 2:4, :].rearrange("p a n -> p (a n)")[:, 0:S + 2 * P]]
        att = rz0[:, :].rearrange("p (c d) -> p c d", c=NC)
        vt = PS[:, 0, :].rearrange("p (c d) -> p c d", c=NC)
        stage = Pt[:, :, :, :].rearrange("p a b n -> p (a b n)")
        raw0 = stage[:, 0:1536]
        rawm = stage[:, 1536:2560].rearrange("p (a b) -> p a b", a=8)
        raw1 = stage[:, 2560:2816].rearrange("p (a b) -> p a b", a=2)
        rawt = stage[0:H1, 2816:3200]
        craw = stage[:, 3200:3200 + 2 * B].rearrange("p (a b) -> p a b", a=2)
        cth = stage[:, 3232:3232 + 2 * B].rearrange("p (a b) -> p a b", a=2)
        t0 = stage[0:H1, 3264:3265]
        tabx = nc.dram_tensor("tabx", (H1, 384), F32).ap()

        ring = [ctx.enter_context(nc.psum_tensor(f"ring{u}", [P, 2, S], F32)) for u in range(NU)]
        O = ctx.enter_context(nc.psum_tensor("O", [P, S], F32))
        Y = ctx.enter_context(nc.psum_tensor("Y", [P, NC, D], F32))

        s_wq = sem("loaded_w0")
        s_small = sem("loaded_small")
        s_w1 = sem("loaded_w1")
        s_mod = sem("loaded_mod")
        s_ffn = sem("loaded_ffn")
        s_tab = sem("loaded_table")
        s_tabx = sem("table_spread")
        s_const = sem("constants")
        s_gconst = sem("pool_constants")
        s_sel = sem("selector_rows")
        s_th = sem("tanh_c")
        s_silu = sem("silu_c")
        s_pm = sem("mod_products")
        s_modc = sem("mod_columns")
        s_wsp = sem("weights_split")
        s_init = sem("vector_init")
        gates_ps = signal("gates_ps", 1)
        ht_ps = signal("ht_ps", 4)
        v0_ps = signal("v0_ps", 2)
        proj0_ps = signal("proj0_ps", PAIRS)
        max0_ps = signal("max0_ps", 4 * PAIRS)
        mt0_ps = signal("mt0_ps", PAIRS)
        sc0_ps = signal("sc0_ps", NC * PAIRS)
        pv0_ps = signal("pv0_ps", NC * PAIRS)
        z0_ps = signal("z0_ps", PAIRS)
        out0_ps = signal("out0_ps", 1)
        gate0_ps = signal("gate0_ps", 1)
        pos_ps = signal("pos_ps", 1)
        v1_ps = signal("v1_ps", 1)
        tv_ps = signal("tv_ps", 1)
        proj1_ps = signal("proj1_ps", G)
        max1_ps = signal("max1_ps", 8 * G)
        mt1_ps = signal("mt1_ps", G)
        sc1_ps = signal("sc1_ps", 2 * NC * G)
        pv1_ps = signal("pv1_ps", NC * G)
        d1_ps = signal("d1_ps", G)
        nat_ps = signal("nat_ps", G)
        route_ps = signal("route_ps", 1)
        gu_ps = signal("gu_ps", NF)
        down_ps = signal("down_ps", NF)
        h32_up = signal("h32_up", 4)
        hhi_up = signal("hhi_up", 3)
        v0_up = signal("v0_up", 2)
        hi0_up = signal("hi0_up", 4 * PAIRS)
        m0_up = signal("m0_up", PAIRS)
        p0_up = signal("p0_up", NC * PAIRS)
        e0_up = signal("e0_up", 1)
        v1_up = signal("v1_up", 1)
        tv_up = signal("tv_up", 1)
        hi1_up = signal("hi1_up", 2 * G)
        m1_up = signal("m1_up", G)
        p1_up = signal("p1_up", 2 * NC * G)
        ot1_up = signal("ot1_up", 2 * G)
        er_up = signal("er_up", 2)
        th_up = signal("th_up", NF)
        gates_up = signal("gates_up", 1)
        ve_up = signal("ve_up", 5)
        nrm_up = signal("nrm_up", 5)
        hlo_up = signal("hlo_up", 3)
        lo0_up = signal("lo0_up", 4 * PAIRS)
        max0_up = signal("max0_up", 4 * PAIRS)
        rz0_up = signal("rz0_up", PAIRS)
        o0_up = signal("o0_up", PAIRS)
        ga0_up = signal("ga0_up", 1)
        d0_up = signal("d0_up", 1)
        cs_up = signal("cs_up", 1)
        kept_up = signal("kept_up", 1)
        y0_up = signal("y0_up", 1)
        lo1_up = signal("lo1_up", 2 * G)
        max1_up = signal("max1_up", 8 * G)
        att_up = signal("att_up", G)
        rt_up = signal("rt_up", 1)
        cw_up = signal("cw_up", 1)
        hs_up = signal("hs_up", NF)
        acc_up = signal("acc_up", E1)
        fout_up = signal("fout_up", 1)
        dve_a = Chain(sem("vector_a"), 45)
        dve_f = Chain(sem("vector_f"), NF + 1)
        sel_up = signal("sel_up", 1)
        modb_up = signal("modb_up", 2)
        xp_up = signal("xp_up", 1)
        rstd_up = signal("rstd_up", 5)
        ps0_up = signal("ps0_up", 3 * PAIRS)
        ones1_up = signal("ones1_up", 1)
        vt_up = signal("vt_up", 1)
        km_up = signal("km_up", HG * G)
        g1_up = signal("g1_up", 1)
        xb_up = signal("xb_up", 1)
        gbf_up = signal("gbf_up", 1)
        ws_up = signal("ws_up", 4 * E1)
        pool_a = Chain(sem("pool_a"), 2)
        hold_a = Chain(sem("pool_hold_a"), 8)
        hold_f = Chain(sem("pool_hold_f"), 14)
        x_in = signal("x_in", 16)
        dup0 = [[signal(f"dup0_{i}{h}", 32 * PAIRS // 2) for h in range(2)] for i in range(2)]
        stored = signal("stored", 16)

        def freed_by(s):
            k = s[0]
            if k == "gates":
                return gates_up, 0, "a"
            if k == "ht":
                return (h32_up, 1, "a") if s[1] == 1 else (hhi_up, {0: 0, 2: 1, 3: 2}[s[1]], "a")
            if k == "v0":
                return v0_up, s[1], "a"
            if k == "proj0":
                return lo0_up, 4 * s[1] + 3, "a"
            if k == "max0":
                return max0_up, 4 * s[1] + s[2], "a"
            if k == "mt0":
                return m0_up, s[1], "a"
            if k == "sc0":
                return p0_up, NC * s[1] + s[2], "a"
            if k == "z0":
                return rz0_up, s[1], "a"
            if k == "out0":
                return ga0_up, 0, "a"
            if k == "gate0":
                return y0_up, 0, "a"
            if k == "pos":
                return kept_up, 0, "a"
            if k == "v1":
                return v1_up, 0, "a"
            if k == "tv":
                return tv_up, 0, "a"
            if k == "proj1":
                return lo1_up, 2 * s[1] + 1, "a"
            if k == "max1":
                return max1_up, 8 * s[1] + s[2], "a"
            if k == "mt1":
                return m1_up, s[1], "a"
            if k == "sc1":
                return p1_up, 2 * (NC * s[1] + s[2]) + s[3], "a"
            if k == "d1":
                return ot1_up, 2 * s[1] + 1, "a"
            if k == "nat":
                return att_up, s[1], "a"
            if k == "route":
                return rt_up, 0, "a"
            return hs_up, s[1], "f"

        first = Phase(A_STEPS, 0, None)
        last = Phase(F_STEPS, None, B - 1)

        def run(eng, parts, chains=()):
            def walk(phase):
                for c in chains:
                    c.start()
                for s in phase.steps:
                    if s[0] in parts:
                        parts[s[0]](phase, *s[1:])

            walk(first)
            with eng.Fori(1, B) as t:
                walk(Phase(LOOP_STEPS, t, t - 1))
            walk(last)

        def unit(ph, *s):
            return ring[ph.slot[s]]

        def as32(ap):
            return ap.bitcast(F32)

        block = ctx.enter_context(nc.Block())

        @block.sync
        def _(sp):
            xv = x.rearrange("b (c p) d -> b p c d", p=P)
            ov = out.rearrange("b (c p) d -> b p c d", p=P)
            sp.dma_start(xin[:, :, :], xv[0]).then_inc(x_in.sem, 16)
            sp.dma_start(craw, cT).then_inc(s_mod, 16)
            sp.dma_start(rawm.rearrange("p (l k) d -> p l k d", l=2)[:, :, 0:2, :],
                         wmod[:, :, 0:2, :]).then_inc(s_mod, 16)
            sp.dma_start(rawm.rearrange("p (l k) d -> p l k d", l=2)[:, :, 2:4, :],
                         wmod[:, :, 3:5, :]).then_inc(s_mod, 16)
            for k in range(2):
                sp.dma_start(wgate[:, :, k, :], wmod[:, :, 2 + 3 * k, :]).then_inc(s_mod, 16)
            sp.dma_start(raw0, wqkv0).then_inc(s_wq, 16)
            for dst, src in ((wo[:, :, :], wout0.rearrange("(a p) d -> p a d", p=P)),
                             (bo[:, :], bout0.partition_broadcast(P)), (wg[:, :], wg0), (we[:, :], we0),
                             (be[:, :], be0), (gam[:, :], gamma.partition_broadcast(P)),
                             (bet[:, :], beta.partition_broadcast(P)),
                             (tlast[:, :], t_last.partition_broadcast(P)), (wv[:, :], wv1T),
                             (wr[:, :, :], wr1)):
                sp.dma_start(dst, src).then_inc(s_small, 16)
            sp.dma_start(raw1, wqk1).then_inc(s_w1, 16)
            sp.wait_ge(s_tab, 1)
            sp.dma_start(rawt[:, P:P + TAB], table).then_inc(s_tabx, 16)
            sp.dma_start(wgu[:, :, :, :], wgu1).then_inc(s_ffn, 16)
            sp.dma_start(wd[:, :, :, :], wd1).then_inc(s_ffn, 16)
            sp.wait_ge(s_tab, 2)
            sp.dma_start(tabx, rawt).then_inc(s_tabx, 16)
            sp.wait_ge(s_tabx, 32)
            sp.dma_start(biasd[:, :, :], bass.AP(tensor=tabx.tensor, offset=0,
                                                 ap=[[1, P], [384, H1], [1, 2 * P]])).then_inc(s_tabx, 16)

            def load(ph):
                t = ph.a
                if isinstance(t, int):
                    return
                nrm_up.wait(sp, t, -5)
                xp_up.wait(sp, t, -1)
                sp.dma_start(xin[:, :, :], xv[t]).then_inc(x_in.sem, 16)

            def proj0(ph, p):
                t, i = ph.a, p % 2
                for h in range(2):
                    r, o = (slice(0, 64), slice(64, 128)) if h == 0 else (slice(64, 128), slice(0, 64))
                    hi0_up.wait(sp, t, 4 * p + h)
                    sp.dma_start(as32(qk[0:64, i, 2, h, :]), as32(qk[r, i, 0, h, :])
                                 ).then_inc(dup0[i][h].sem, 16)
                    hi0_up.wait(sp, t, 4 * p + 2 + h)
                    sp.dma_start(as32(qk[o, i, 1, h, :]), as32(qk[r, i, 1, h, :])
                                 ).then_inc(dup0[i][h].sem, 16)

            def down(ph, n):
                if n == NF - 1:
                    fout_up.wait(sp, ph.f, 0)
                    sp.dma_start(ov[ph.f], acc[:, :, :]).then_inc(stored.sem, 16)

            run(sp, {"load": load, "proj0": proj0, "down": down})
            sp.wait_ge(stored.sem, 16 * B)

        @block.gpsimd
        def _(pool):
            pool.memset(ident[:, :], 0.0).then_inc(s_gconst, 1)
            pool.memset(upper[:, :], 1.0).then_inc(s_gconst, 1)
            pool.memset(mask[:, :], 1.0).then_inc(s_gconst, 1)
            pool.wait_ge(s_gconst, 3)
            pool.affine_select(out=ident[:, :], in_=ident[:, :], compare_op=ALU.not_equal, fill=1.0,
                               base=0, pattern=[[-1, P]], channel_multiplier=1).then_inc(s_gconst, 1)
            pool.affine_select(out=upper[:, :], in_=upper[:, :], compare_op=ALU.is_ge, fill=0.0,
                               base=0, pattern=[[1, P]], channel_multiplier=-1).then_inc(s_gconst, 1)
            for qd in range(3):
                for lo in (True, False):
                    mk = mask[QR * qd:QR * qd + QR, :]
                    pool.affine_select(out=mk, in_=mk, compare_op=ALU.is_ge, fill=0.0,
                                       base=0 if lo else DH1 - 1, pattern=[[-DH1 if lo else DH1, HG]],
                                       channel_multiplier=1 if lo else -1).then_inc(s_gconst, 1)
                    pool.wait_ge(s_gconst, 6 + 2 * qd + (not lo))
            pool.memset(neghalf[:, :], -0.5).then_inc(s_gconst, 1)
            for e in range(E0):
                pool.memset(rev[:, e:e + 1], float(E0 - e)).then_inc(s_gconst, 1)
            pool.memset(cs[:, 0, :], 0.0).then_inc(s_gconst, 1)
            pool.memset(rawt, 0.0).then_inc(s_tab, 1)

            def hold(chain, batch):
                if chain.n:
                    chain.wait(pool, batch)
                k = int(chain is hold_f)
                chain.link(pool.tensor_tensor(idle[0:1, k:k + 1], neghalf[0:1, 0:1], neghalf[0:1, 0:1],
                                              ALU.mult))

            def gates_step(ph):
                t = ph.a
                if isinstance(t, int):
                    pool.wait_ge(s_modc, 2)
                    pool.wait_ge(s_gconst, 23)
                sc1_ps.wait(pool, t, -1)
                hold(hold_a, ph.a)
                pool.tensor_copy(qk[0:96, :, 3, :, :], ident[0:96, 64:66].unsqueeze(1).unsqueeze(3)
                                 .broadcast_to([96, 2, 2, S])).then_inc(sel_up.sem, 1)
                gates_ps.wait(pool, t, -1)
                hhi_up.wait(pool, t, -1)
                hold(hold_a, ph.a)
                pool.tensor_copy(scb[:, :, :], sT[:, :, bass.ds(t, 1)].broadcast_to([P, 2, P])
                                 ).then_inc(modb_up.sem, 1)
                pool.tensor_copy(modb[:, :].unsqueeze(2), modc[:, :, bass.ds(t, 1)]).then_inc(modb_up.sem, 1)
                gates_up.wait(pool, t, 0)
                x_in.wait(pool, t, 15)
                if isinstance(t, int):
                    pool.wait_ge(s_small, 160)
                pool.tensor_tensor(gbo[:, :], gates[:, 0, :], bo[:, :], ALU.mult).then_inc(pool_a.sem, 1)
                pool_a.n += 1
                pool_a.wait(pool, t)
                pool.tensor_tensor(xres[:, :, :], xin[:, :, :], gbo[:, :].unsqueeze(1).broadcast_to([P, NC, D]),
                                   ALU.add).then_inc(xp_up.sem, 1)

            def ln(ph, n):
                ve_up.wait(pool, ph.a, n)
                pool.tensor_tensor(rstd[:, :], ve[:, :], neghalf[:, :], ALU.pow).then_inc(rstd_up.sem, 1)

            def pv0(ph, p, jc):
                t = ph.a
                if jc == 0:
                    return
                p0_up.wait(pool, t, NC * p + jc)
                if jc == 1:
                    if p:
                        z0_ps.wait(pool, t, p - 1)
                    pool.tensor_tensor(PS[:, :, :], Pt[:, 0, :, :], Pt[:, 1, :, :], ALU.add
                                       ).then_inc(ps0_up.sem, 1)
                else:
                    ps0_up.wait(pool, t, 3 * p + jc - 2)
                    pool.tensor_tensor(PS[:, :, :], PS[:, :, :], Pt[:, jc, :, :], ALU.add
                                       ).then_inc(ps0_up.sem, 1)

            def out0(ph):
                out0_ps.wait(pool, ph.a)
                hold(hold_a, ph.a)
                pool.memset(V1[:, :, :, DH1:], 1.0).then_inc(ones1_up.sem, 1)

            def v1(ph):
                t = ph.a
                v1_up.wait(pool, t)
                pool.tensor_tensor(vt.rearrange("p c (h m) -> p c h m", h=H1), V1[:, :, :, 0:DH1],
                                   t254[:, :, :].unsqueeze(1).broadcast_to([P, NC, H1, DH1]),
                                   ALU.mult).then_inc(vt_up.sem, 1)
                pool.tensor_tensor(g1[:, :], gates[:, 2, :], gam[:, :], ALU.mult).then_inc(g1_up.sem, 1)
                pool.tensor_tensor(gbo[:, :], gates[:, 2, :], bet[:, :], ALU.mult).then_inc(pool_a.sem, 1)
                pool_a.n += 1
                pool_a.wait(pool, t)
                nrm_up.wait(pool, t, 2)
                pool.tensor_tensor(xres[:, :, :], xres[:, :, :],
                                   gbo[:, :].unsqueeze(1).broadcast_to([P, NC, D]), ALU.add
                                   ).then_inc(xb_up.sem, 1)

            def proj1(ph, g):
                t = ph.a
                lo1_up.wait(pool, t, 2 * g + 1)
                hold(hold_a, ph.a)
                for h in range(HG):
                    pool.tensor_scalar(K1[g % 2][0:96, h, :], as32(ks[:, :]), mask[:, h:h + 1], 1.0,
                                       ALU.mult, ALU.mult).then_inc(km_up.sem, 1)

            def post1(ph):
                ln(ph, 3)

            def route(ph):
                t = ph.a
                if isinstance(t, int):
                    pool.wait_ge(s_ffn, 32)
                else:
                    stored.wait(pool, t, -1)
                hold(hold_a, ph.a)
                pool.tensor_copy(gbf[:, :], gates[:, 3, :]).then_inc(gbf_up.sem, 1)

            def gu(ph, n):
                f = ph.f
                for m in ((0, 2) if n == 0 else (n + 2,)):
                    if m % 2 or m >= NF:
                        continue
                    e, q, i = m // 4, (m // 2) % 2, (m // 2) % 2
                    if m >= 4:
                        gu_ps.wait(pool, f, m - 3)
                        hold(hold_f, f)
                    src = wgu[:, e, :, q * 256:(q + 1) * 256]
                    pool.tensor_copy(ws[:, i, 0, :, :], src).then_inc(ws_up.sem, 1)
                    ws_up.wait(pool, f, m)
                    pool.tensor_tensor(ws[:, i, 1, :, :], src, as32(ws[:, i, 0, :, :]), ALU.subtract
                                       ).then_inc(ws_up.sem, 1)

            pool.wait_ge(s_gconst, 21)
            for i in range(2):
                pool.wait_ge(s_sel, i + 1)
                pool.tensor_copy(K1[i][96:128, :, :],
                                 ident[96:128, 96:96 + HG].unsqueeze(2).broadcast_to([32, HG, S])
                                 ).then_inc(s_gconst, 1)
            run(pool, {"gates": gates_step, "ln": ln, "pv0": pv0, "out0": out0, "v1": v1, "proj1": proj1,
                       "post1": post1, "route": route, "gu": gu}, [pool_a, hold_a, hold_f])

        @block.scalar
        def _(act):
            ID, EXP, TANH, COPY = ACT.Identity, ACT.Exp, ACT.Tanh, ACT.Copy
            act.wait_ge(s_mod, 80)
            act.activation(cth, craw, TANH, scale=0.5).then_inc(s_th, 1)

            def ht(ph, l):
                t = ph.a
                ht_ps.wait(act, t, l)
                if l == 0:
                    modb_up.wait(act, t, 1)
                u = unit(ph, "ht", l)
                k = 2 * l
                s, c = modb[:, k:k + 1], modb[:, k + 1:k + 2]
                if l == 3 and not isinstance(t, int):
                    fout_up.wait(act, t, -1)
                act.activation(h32[:, :], u[:, 0, :], ID, bias=s, scale=c).then_inc(h32_up.sem, 1)
                if l != 1:
                    dst = fT if l == 3 else hT
                    act.activation(dst[:, 0, :], u[:, 0, :], ID, bias=s, scale=c).then_inc(hhi_up.sem, 1)

            def v0(ph, i):
                v0_ps.wait(act, ph.a, i)
                act.activation(V[:, 2 * i:2 * i + 2, :], unit(ph, "v0", i)[:, :, :], COPY).then_inc(v0_up.sem, 1)

            def proj0(ph, p):
                proj0_ps.wait(act, ph.a, p)
                u, i = unit(ph, "proj0", p), p % 2
                for k in range(2):
                    for h in range(2):
                        r = slice(64 * h, 64 * h + 64)
                        act.activation(qk[r, i, k, h, :], u[r, k, :], COPY).then_inc(hi0_up.sem, 1)

            def mt0(ph, p):
                mt0_ps.wait(act, ph.a, p)
                u = unit(ph, "mt0", p)
                act.activation(qk[64:66, p % 2, 2, :, :], u[0:2, 0, :].unsqueeze(1).broadcast_to([2, 2, S]),
                               COPY).then_inc(m0_up.sem, 1)

            def sc0(ph, p, jc):
                t = ph.a
                sc0_ps.wait(act, t, NC * p + jc)
                if p:
                    pv0_ps.wait(act, t, NC * (p - 1) + jc)
                    ps0_up.wait(act, t, 3 * (p - 1) + max(jc - 1, 0))
                act.activation(Pt[:, jc, :, :], unit(ph, "sc0", p, jc)[:, :, :], EXP,
                               scale=SCALE0).then_inc(p0_up.sem, 1)

            def gate0(ph):
                d0_up.wait(act, ph.a)
                act.activation(sm2[:, :, 0, :], sm[:, :, 0, :], EXP).then_inc(e0_up.sem, 1)

            def v1(ph):
                v1_ps.wait(act, ph.a)
                u = unit(ph, "v1")
                act.activation(V1[:, :, :, 0:DH1], u[:, 0, :].rearrange("p (c h m) -> p c h m", c=NC, h=H1),
                               COPY).then_inc(v1_up.sem, 1)

            def tv_step(ph):
                tv_ps.wait(act, ph.a)
                act.activation(tv[:, :], unit(ph, "tv")[:, 0, 0:D], COPY).then_inc(tv_up.sem, 1)

            def proj1(ph, g):
                t = ph.a
                proj1_ps.wait(act, t, g)
                u = unit(ph, "proj1", g)
                act.activation(X1[g % 2][0:96, :], u[0:96, 0, :], COPY).then_inc(hi1_up.sem, 1)
                if g:
                    km_up.wait(act, t, HG * g - 1)
                act.activation(ks[:, :], u[0:96, 1, :], COPY).then_inc(hi1_up.sem, 1)

            def mt1(ph, g):
                mt1_ps.wait(act, ph.a, g)
                act.activation(X1[g % 2][96:100, :], unit(ph, "mt1", g)[0:4, 0, :], COPY).then_inc(m1_up.sem, 1)

            def sc1(ph, g, jc, hp):
                t, n = ph.a, 2 * (NC * g + jc) + hp
                sc1_ps.wait(act, t, n)
                if n >= 4:
                    pv1_ps.wait(act, t, (n - 4) // 2)
                act.activation(Pt[:, n % 4, :, :], unit(ph, "sc1", g, jc, hp)[:, :, :], EXP,
                               scale=SCALE1).then_inc(p1_up.sem, 1)

            def d1(ph, g):
                t = ph.a
                pv1_ps.wait(act, t, NC * g + NC - 1)
                act.activation(OT[g % 2][:, 0:S], O[:, :], COPY).then_inc(ot1_up.sem, 1)
                d1_ps.wait(act, t, g)
                act.activation(OT[g % 2][:, S:S + 2 * P], unit(ph, "d1", g)[:, 0, 2 * P - 1::-1], COPY).then_inc(ot1_up.sem, 1)

            def route(ph):
                t = ph.a
                rt_up.wait(act, t)
                act.activation(sm2[:, :, 0, :], sm[:, :, 0, :], EXP).then_inc(er_up.sem, 1)
                act.activation(sm2[:, :, 1, :], sm[:, :, 1, :], EXP, scale=1.0 / TEMP).then_inc(er_up.sem, 1)

            def gu(ph, n):
                f = ph.f
                gu_ps.wait(act, f, n)
                if n >= 4:
                    down_ps.wait(act, f, n - 4)
                act.activation(hs[:, n % 4, :], unit(ph, "gu", n)[:, 0, :], TANH, scale=0.5).then_inc(th_up.sem, 1)

            run(act, {"ht": ht, "v0": v0, "proj0": proj0, "mt0": mt0, "sc0": sc0, "gate0": gate0, "v1": v1,
                      "tv": tv_step, "proj1": proj1, "mt1": mt1, "sc1": sc1, "d1": d1, "route": route, "gu": gu})

        @block.vector
        def _(dve):
            dve.memset(ones[:, :], 1.0).then_inc(s_const, 1)
            for i in range(2):
                dve.memset(as32(qk[:, i, :, :, :]), 0.0).then_inc(s_sel, 1)
            dve.wait_ge(s_th, 1)
            dve.scalar_tensor_tensor(cth, cth, 1.0, craw, ALU.add, ALU.mult).then_inc(s_silu, 1)
            dve.wait_ge(s_silu, 1)
            dve.tensor_scalar(sT[:, :, :], cth, 0.5, None, ALU.mult).then_inc(s_silu, 1)
            dve.wait_ge(s_wq, 16)
            dve.tensor_copy(w0[:, 0, :], raw0).then_inc(s_wsp, 1)
            dve.wait_ge(s_wsp, 1)
            dve.tensor_tensor(w0[:, 1, :], raw0, as32(w0[:, 0, :]), ALU.subtract).then_inc(s_wsp, 1)
            dve.wait_ge(s_w1, 16)
            for k in range(2):
                r = raw1[:, k, :].rearrange("p (g m) -> p g m", g=G).unsqueeze(2).broadcast_to([P, G, 3, QR])
                dve.tensor_copy(w1[:, 0, k, :, :, :], r).then_inc(s_wsp, 1)
                dve.wait_ge(s_wsp, 3 + 2 * k)
                dve.tensor_tensor(w1[:, 1, k, :, :, :], r, as32(w1[:, 0, k, :, :, :]), ALU.subtract
                                  ).then_inc(s_wsp, 1)
            dve.wait_ge(s_pm, 1)
            mp = ring[0][:, 0, 0:8 * B].rearrange("p (k b) -> p k b", k=8)
            dve.tensor_copy(modc[:, 0::2, :], mp[:, 0::2, :]).then_inc(s_modc, 1)
            dve.tensor_scalar(modc[:, 1::2, :], mp[:, 1::2, :], 1.0, None, ALU.add).then_inc(s_modc, 1)
            dve.wait_ge(s_tabx, 16)
            dve.tensor_copy(t0, rawt[:, P:P + 1]).then_inc(s_init, 1)
            dve.wait_ge(s_init, 1)
            dve.tensor_scalar(rawt[:, P:P + TAB], rawt[:, P:P + TAB], t0, None, ALU.subtract).then_inc(s_tab, 1)
            dve.wait_ge(s_small, 160)
            dve.tensor_copy(t254[:, :, :], tlast[:, :].unsqueeze(2).broadcast_to([P, H1, DH1])).then_inc(s_init, 1)

            A = dve_a

            def gates_step(ph):
                t = ph.a
                gates_ps.wait(dve, t)
                xb_up.wait(dve, t, -1)
                gbf_up.wait(dve, t, -1)
                gp = unit(ph, "gates")[:, 0, :].rearrange("p (k d) -> p k d", k=4)
                A.link(dve.tensor_scalar(nrm[:, :, :], gp, 0.0, 0.5, ALU.is_ge, ALU.subtract))
                A.wait(dve, t)
                A.link(dve.scalar_tensor_tensor(gates[:, :, :], nrm[:, :, :], 4.0, gp, ALU.mult, ALU.mult))
                A.wait(dve, t)
                dve.scalar_tensor_tensor(gates[:, :, :], gates[:, :, :], 0.5, nrm[:, :, :], ALU.max,
                                         ALU.mult).then_inc(gates_up.sem, 1)

            def ln(ph, n):
                t = ph.a
                if n == 0:
                    x_in.wait(dve, t, 15)
                if n == 3:
                    src = att
                elif n == 4:
                    src = xf
                else:
                    src = xin if n == 0 else xres
                for c in range(NC):
                    i = dve.bn_stats(st[:, c, :], src[:, c, :])
                A.link(i)
                A.wait(dve, t)
                dve.tensor_copy(ve[0:1, 0:1], st[0:1, 0, 0:1])
                for c in range(NC):
                    i = dve.bn_aggr(mv[:, c, :], st[:, c, :])
                A.link(i)
                A.wait(dve, t)
                dve.tensor_scalar(ve[:, :], mv[:, :, 1], EPS, None, ALU.add).then_inc(ve_up.sem, 1)
                rstd_up.wait(dve, t, n)
                for c in range(NC):
                    i = dve.tensor_scalar(nrm[:, c, :], src[:, c, :], mv[:, c, 0:1], rstd[:, c:c + 1],
                                          ALU.subtract, ALU.mult)
                i.then_inc(nrm_up.sem, 1)

            def ht(ph, l):
                t = ph.a
                if l == 1:
                    return
                k = {0: 0, 2: 1, 3: 2}[l]
                hhi_up.wait(dve, t, k)
                dst = fT if l == 3 else hT
                dve.tensor_tensor(dst[:, 1, :], h32[:, :], as32(dst[:, 0, :]), ALU.subtract
                                  ).then_inc(hlo_up.sem, 1)

            def proj0(ph, p):
                t, i = ph.a, p % 2
                u = unit(ph, "proj0", p)
                for h in range(2):
                    r, o = (slice(0, 64), slice(64, 128)) if h == 0 else (slice(64, 128), slice(0, 64))
                    hi0_up.wait(dve, t, 4 * p + h)
                    dve.tensor_tensor(qk[o, i, 0, h, :], u[r, 0, :], as32(qk[r, i, 0, h, :]), ALU.subtract
                                      ).then_inc(lo0_up.sem, 1)
                for h in range(2):
                    r = slice(64 * h, 64 * h + 64)
                    hi0_up.wait(dve, t, 4 * p + 2 + h)
                    if p == 0 and h == 0:
                        sel_up.wait(dve, t)
                    dve.tensor_tensor(qk[0:64, i, 3, h, :], u[r, 1, :], as32(qk[r, i, 1, h, :]), ALU.subtract
                                      ).then_inc(lo0_up.sem, 1)

            def max0(ph, p, k):
                t = ph.a
                h, half = k // 2, k % 2
                max0_ps.wait(dve, t, 4 * p + k)
                dve.tensor_reduce(nm0[:, p % 2, 2 * half:2 * half + 2, h], unit(ph, "max0", p, k)[:, :, :], X,
                                  ALU.max, negate=True).then_inc(max0_up.sem, 1)

            def z0(ph, p):
                t = ph.a
                z0_ps.wait(dve, t, p)
                dve.reciprocal(rz0[:, :], unit(ph, "z0", p)[:, 0, :]).then_inc(rz0_up.sem, 1)
                rz0_up.wait(dve, t, p)
                dve.tensor_tensor(oT[:, p, :], O[:, :], rz0[:, :], ALU.mult).then_inc(o0_up.sem, 1)

            def wide(g):
                return g.unsqueeze(1).broadcast_to([P, NC, D])

            def out0(ph):
                t = ph.a
                out0_ps.wait(dve, t)
                y = unit(ph, "out0")[:, 0, :].rearrange("p (c d) -> p c d", c=NC)
                dve.tensor_tensor(nrm[:, :, :], y, wide(gates[:, 0, :]), ALU.mult).then_inc(ga0_up.sem, 1)
                ga0_up.wait(dve, t)
                xp_up.wait(dve, t)
                A.link(dve.tensor_tensor(xres[:, :, :], xres[:, :, :], nrm[:, :, :], ALU.add))
                A.wait(dve, t)

            def w8(ap):
                return ap.unsqueeze(2).broadcast_to([P, NC, E0])

            def gate0(ph):
                t = ph.a
                gate0_ps.wait(dve, t)
                lg = unit(ph, "gate0")[:, 0, 0:NC * E0].rearrange("p (c e) -> p c e", c=NC)
                A.link(dve.tensor_reduce(sc4[:, 0, :], lg, X, ALU.max))
                A.wait(dve, t)
                dve.tensor_tensor(sm[:, :, 0, :], lg, w8(sc4[:, 0, :]), ALU.subtract).then_inc(d0_up.sem, 1)
                d0_up.wait(dve, t)
                A.link(dve.scalar_tensor_tensor(sm3[:, :, :], sm[:, :, 0, :], 0.0,
                                                rev[:, :].unsqueeze(1).broadcast_to([P, NC, E0]),
                                                ALU.is_equal, ALU.mult))
                A.wait(dve, t)
                A.link(dve.tensor_reduce(sc4[:, 1, :], sm3[:, :, :], X, ALU.max))
                A.wait(dve, t)
                A.link(dve.tensor_tensor(oh[:, :, :], sm3[:, :, :], w8(sc4[:, 1, :]), ALU.is_equal))
                A.wait(dve, t)
                for c in range(1, NC):
                    i = dve.tensor_tensor(cs[:, c, :], cs[:, c - 1, :], oh[:, c - 1, :], ALU.add)
                    if c < NC - 1:
                        A.link(i)
                        A.wait(dve, t)
                i.then_inc(cs_up.sem, 1)
                e0_up.wait(dve, t)
                A.link(dve.tensor_reduce(sc4[:, 2, :], sm2[:, :, 0, :], X, ALU.add))
                A.wait(dve, t)
                A.link(dve.reciprocal(sc4[:, 3, :], sc4[:, 2, :]))

            def pos(ph):
                t = ph.a
                pos_ps.wait(dve, t)
                ps = unit(ph, "pos")[:, 0, 0:NC * E0].rearrange("p (c e) -> p c e", c=NC)
                dve.scalar_tensor_tensor(sm3[:, :, :], ps, float(CAP), oh[:, :, :], ALU.is_le, ALU.mult
                                         ).then_inc(kept_up.sem, 1)
                A.link(dve.tensor_tensor(cs[:, 0, :], cs[:, NC - 1, :], oh[:, NC - 1, :], ALU.add))
                kept_up.wait(dve, t)
                A.link(dve.tensor_reduce(sc4[:, 4, :], sm3[:, :, :], X, ALU.add))
                A.wait(dve, t)
                A.link(dve.tensor_tensor(sc4[:, 5, :], sc4[:, 4, :], sc4[:, 3, :], ALU.mult))
                A.wait(dve, t)
                y = unit(ph, "gate0")[:, 1, :].rearrange("p (c d) -> p c d", c=NC)
                for c in range(NC):
                    i = dve.scalar_tensor_tensor(nrm[:, c, :], y[:, c, :], sc4[:, 5, c:c + 1], gates[:, 1, :],
                                                 ALU.mult, ALU.mult)
                i.then_inc(y0_up.sem, 1)
                y0_up.wait(dve, t)
                A.link(dve.tensor_tensor(xres[:, :, :], xres[:, :, :], nrm[:, :, :], ALU.add))
                A.wait(dve, t)

            def proj1(ph, g):
                t = ph.a
                u = unit(ph, "proj1", g)
                hi1_up.wait(dve, t, 2 * g)
                dve.tensor_tensor(X1[g % 2][32:64, :], u[32:64, 0, :], as32(X1[g % 2][32:64, :]), ALU.subtract
                                  ).then_inc(lo1_up.sem, 1)
                hi1_up.wait(dve, t, 2 * g + 1)
                dve.tensor_tensor(ks[64:96, :], u[64:96, 1, :], as32(ks[64:96, :]), ALU.subtract
                                  ).then_inc(lo1_up.sem, 1)

            def max1(ph, g, k):
                t = ph.a
                h, half = k // 2, k % 2
                max1_ps.wait(dve, t, 8 * g + k)
                dve.tensor_reduce(nm1[:, g % 2, 2 * half:2 * half + 2, h], unit(ph, "max1", g, k)[:, :, :], X,
                                  ALU.max, negate=True).then_inc(max1_up.sem, 1)

            def nat(ph, g):
                t = ph.a
                nat_ps.wait(dve, t, g)
                u = unit(ph, "nat", g)
                o = u[:, 0, :].rearrange("p (c q m) -> p c q m", c=NC, q=HG)
                d = u[:, 1, 0:2 * P].rearrange("p (c q m) -> p c q m", c=2, q=HG)
                a = att[:, :, QR * g:QR * g + QR].rearrange("p c (q m) -> p c q m", q=HG)
                A.link(dve.reciprocal(rz1[:, :, :], o[:, :, :, DH1]))
                A.wait(dve, t)
                A.link(dve.tensor_tensor(a, o[:, :, :, 0:DH1],
                                         rz1[:, :, :].unsqueeze(3).broadcast_to([P, NC, HG, DH1]), ALU.mult))
                A.wait(dve, t)
                dve.tensor_tensor(a[:, 0:2], a[:, 0:2], d[:, :, :, 0:DH1], ALU.add).then_inc(att_up.sem, 1)

            def post1(ph):
                t = ph.a
                tv_up.wait(dve, t)
                att_up.wait(dve, t, G - 1)
                A.link(dve.tensor_tensor(att, att, wide(tv[:, :]), ALU.add))
                A.wait(dve, t)
                ln(ph, 3)
                nrm_up.wait(dve, t, 3)
                g1_up.wait(dve, t)
                A.link(dve.tensor_tensor(nrm[:, :, :], nrm[:, :, :], wide(g1[:, :]), ALU.mult))
                A.wait(dve, t)
                xb_up.wait(dve, t)
                if not isinstance(t, int):
                    fout_up.wait(dve, t, -1)
                A.link(dve.tensor_tensor(xf[:, :, :], nrm[:, :, :], xres[:, :, :], ALU.add))
                A.wait(dve, t)

            def route(ph):
                t = ph.a
                route_ps.wait(dve, t)
                lg = unit(ph, "route")[:, 0, 0:NC * 2 * E1].rearrange("p (c k e) -> p (c k) e", c=NC, k=2)
                d = sm[:, :, :, :].rearrange("p c k e -> p (c k) e")
                A.link(dve.tensor_reduce(sc4[:, 0:2, :].rearrange("p a c -> p (a c)"), lg, X, ALU.max))
                A.wait(dve, t)
                dve.tensor_tensor(d, lg, sc4[:, 0:2, :].rearrange("p a c -> p (a c)").unsqueeze(2)
                                  .broadcast_to([P, 2 * NC, E1]), ALU.subtract).then_inc(rt_up.sem, 1)
                er_up.wait(dve, t, 1)
                s2 = sc4[:, 2:4, :].rearrange("p a c -> p (a c)")
                A.link(dve.tensor_reduce(s2, sm2[:, :, :, :].rearrange("p c k e -> p (c k) e"), X, ALU.add))
                A.link(dve.tensor_tensor(sm3[:, :, :], sm2[:, :, 0, :], sm2[:, :, 1, :], ALU.mult))
                A.wait(dve, t)
                A.link(dve.reciprocal(s2, s2))
                A.wait(dve, t)
                s2v = s2.rearrange("p (c k) -> p c k", k=2)
                A.link(dve.tensor_tensor(sc4[:, 4, :], s2v[:, :, 0], s2v[:, :, 1], ALU.mult))
                A.wait(dve, t)
                A.link(dve.tensor_tensor(sm3[:, :, :], sm3[:, :, :], w8(sc4[:, 4, :]), ALU.mult))
                A.wait(dve, t)
                A.link(dve.tensor_reduce(sc4[:, 5, :], sm3[:, :, :], X, ALU.add))
                A.wait(dve, t)
                A.link(dve.tensor_scalar(sc4[:, 5, :], sc4[:, 5, :], 1e-9, None, ALU.add))
                A.wait(dve, t)
                A.link(dve.reciprocal(sc4[:, 6, :], sc4[:, 5, :]))
                A.wait(dve, t)
                dve.tensor_tensor(cw[:, :, :], sm3[:, :, :], w8(sc4[:, 6, :]), ALU.mult).then_inc(cw_up.sem, 1)
                A.end()

            def gu(ph, n):
                f = ph.f
                u = unit(ph, "gu", n)
                s = hs[:, n % 4, :]
                th_up.wait(dve, f, n)
                dve_f.link(dve.scalar_tensor_tensor(s, s, 1.0, u[:, 0, :], ALU.add, ALU.mult))
                dve_f.wait(dve, f)
                dve.scalar_tensor_tensor(s, s, 0.5, u[:, 1, :], ALU.mult, ALU.mult).then_inc(hs_up.sem, 1)

            def down(ph, n):
                f, e = ph.f, n // FC
                if n % FC != FC - 1:
                    return
                down_ps.wait(dve, f, n)
                if e == 0:
                    cw_up.wait(dve, f)
                    gbf_up.wait(dve, f)
                else:
                    acc_up.wait(dve, f, e - 1)
                for c in range(NC):
                    if e == 0:
                        i = dve.tensor_scalar(acc[:, c, :], Y[:, c, :], cw[:, c, e:e + 1], None, ALU.mult)
                    else:
                        i = dve.scalar_tensor_tensor(acc[:, c, :], Y[:, c, :], cw[:, c, e:e + 1], acc[:, c, :],
                                                     ALU.mult, ALU.add)
                i.then_inc(acc_up.sem, 1)
                if e == E1 - 1:
                    acc_up.wait(dve, f, e)
                    dve_f.link(dve.tensor_tensor(acc[:, :, :], acc[:, :, :], wide(gbf[:, :]), ALU.mult))
                    dve_f.wait(dve, f)
                    dve.tensor_tensor(acc[:, :, :], acc[:, :, :], xf[:, :, :], ALU.add).then_inc(fout_up.sem, 1)
                    dve_f.end()

            run(dve, {"gates": gates_step, "ln": ln, "ht": ht, "proj0": proj0, "max0": max0, "z0": z0,
                      "out0": out0, "gate0": gate0, "pos": pos, "proj1": proj1, "max1": max1, "nat": nat,
                      "post1": post1, "route": route, "gu": gu, "down": down}, [dve_a, dve_f])

        @block.tensor
        def _(pe):
            def mm(o, lhsT, rhs, start=True, stop=True, **k):
                return pe.matmul(o, lhsT, rhs, start=start, stop=stop, **k)

            pe.wait_ge(s_silu, 2)
            pe.wait_ge(s_mod, 80)
            mp = ring[0][:, 0, 0:8 * B].rearrange("p (k b) -> p k b", k=8)
            for k in range(8):
                i = mm(mp[:, k, :], rawm[:, k, :], sT[:, k // 4, :])
            i.then_inc(s_pm, 1)
            pe.wait_ge(s_modc, 2)
            pe.wait_ge(s_gconst, 23)
            pe.wait_ge(s_const, 1)
            pe.wait_ge(s_small, 160)
            pe.wait_ge(s_wsp, 6)

            def claim(ph, *s):
                prev, a, f = ph.before[s], ph.a, ph.f
                if prev is not None:
                    sig, n, stage = freed_by(prev)
                    sig.wait(pe, a if stage == "a" else f, n)
                elif ph is not first:
                    sig, n, stage = freed_by(first.last[ph.slot[s]])
                    if ph.a is None:
                        sig.wait(pe, B - 1, n)
                    else:
                        sig.wait(pe, ph.a, n - sig.per)
                return ring[ph.slot[s]]

            def split3(o, w_hi, w_lo, m_hi, m_lo):
                mm(o, w_hi, m_hi, stop=False)
                mm(o, w_lo, m_hi, start=False, stop=False)
                return mm(o, w_hi, m_lo, start=False)

            def gates_step(ph):
                t = ph.a
                u = claim(ph, "gates")
                modb_up.wait(pe, t, 0)
                for l in range(2):
                    i = mm(u[:, 0, 256 * l:256 * l + 256], scb[:, l, :],
                           wgate[:, l, :, :].rearrange("p k d -> p (k d)"))
                i.then_inc(gates_ps.sem, 1)

            def ht(ph, l):
                u = claim(ph, "ht", l)
                nrm_up.wait(pe, ph.a, (0, 1, 2, 4)[l])
                for c in range(NC):
                    i = pe.transpose(u[:, 0, c * P:(c + 1) * P], nrm[:, c, :], ident[:, :])
                i.then_inc(ht_ps.sem, 1)

            def v0(ph, i2):
                t = ph.a
                u = claim(ph, "v0", i2)
                hlo_up.wait(pe, t, 0)
                for k in range(2):
                    c = 2 * i2 + k
                    hi, lo = hT[:, 0, c * P:(c + 1) * P], hT[:, 1, c * P:(c + 1) * P]
                    i = split3(u[:, k, :], hi, lo, w0[:, 0, 1024:], w0[:, 1, 1024:])
                i.then_inc(v0_ps.sem, 1)

            def proj0(ph, p):
                t = ph.a
                u = claim(ph, "proj0", p)
                hlo_up.wait(pe, t, 0)
                for k in range(2):
                    cols = slice(512 * k + 128 * p, 512 * k + 128 * p + 128)
                    i = split3(u[:, k, :], w0[:, 0, cols], w0[:, 1, cols], hT[:, 0, :], hT[:, 1, :])
                i.then_inc(proj0_ps.sem, 1)

            def max0(ph, p, k):
                t, b = ph.a, p % 2
                u = claim(ph, "max0", p, k)
                h, half = k // 2, k % 2
                lo0_up.wait(pe, t, 4 * p + h)
                dup0[b][h].wait(pe, t, 32 * (p // 2) + 31)
                for j in range(2):
                    c = 2 * half + j
                    i = mm(u[:, j, :], qk[:, b, 0, h, c * P:(c + 1) * P], qk[:, b, 1, h, :])
                i.then_inc(max0_ps.sem, 1)

            def mt0(ph, p):
                u = claim(ph, "mt0", p)
                max0_up.wait(pe, ph.a, 4 * p + 3)
                for c in range(NC):
                    i = pe.transpose(u[0:2, 0, c * P:(c + 1) * P], nm0[:, p % 2, c, :], ident[:, :])
                i.then_inc(mt0_ps.sem, 1)

            def sc0(ph, p, jc):
                t, b = ph.a, p % 2
                u = claim(ph, "sc0", p, jc)
                m0_up.wait(pe, t, p)
                lo0_up.wait(pe, t, 4 * p + 3)
                if p == 0 and jc == 0:
                    sel_up.wait(pe, t)
                for h in range(2):
                    c = slice(jc * P, (jc + 1) * P)
                    mm(u[:, h, :], qk[:, b, 1, h, c], qk[:, b, 0, h, :], stop=False)
                    i = mm(u[:, h, :], qk[0:96, b, 3, h, c], qk[0:96, b, 2, h, :], start=False)
                i.then_inc(sc0_ps.sem, 1)

            def pv0(ph, p, jc):
                t = ph.a
                p0_up.wait(pe, t, NC * p + jc)
                if p == 0:
                    v0_up.wait(pe, t, jc // 2)
                if jc == 0 and p:
                    o0_up.wait(pe, t, p - 1)
                for h in range(2):
                    i = mm(O[64 * h:64 * h + 64, :], V[:, jc, 128 * p + 64 * h:128 * p + 64 * h + 64],
                           Pt[:, jc, h, :], start=jc == 0, stop=jc == NC - 1)
                i.then_inc(pv0_ps.sem, 1)

            def z0(ph, p):
                t = ph.a
                u = claim(ph, "z0", p)
                ps0_up.wait(pe, t, 3 * p + 2)
                for h in range(2):
                    i = mm(u[64 * h:64 * h + 64, 0, :], ones[:, 0:64], PS[:, h, :])
                i.then_inc(z0_ps.sem, 1)

            def out0(ph):
                t = ph.a
                u = claim(ph, "out0")
                o0_up.wait(pe, t, PAIRS - 1)
                for c in range(NC):
                    for p in range(PAIRS):
                        i = mm(u[:, 0, c * P:(c + 1) * P], oT[:, p, c * P:(c + 1) * P], wo[:, p, :],
                               start=p == 0, stop=p == PAIRS - 1)
                i.then_inc(out0_ps.sem, 1)

            def gate0(ph):
                t = ph.a
                u = claim(ph, "gate0")
                h32_up.wait(pe, t, 1)
                for c in range(NC):
                    mm(u[:, 0, c * E0:(c + 1) * E0], h32[:, c * P:(c + 1) * P], wg[:, :])
                for c in range(NC):
                    mm(u[:, 1, c * P:(c + 1) * P], ones[0:1, :], be[0:1, :], stop=False)
                    i = mm(u[:, 1, c * P:(c + 1) * P], h32[:, c * P:(c + 1) * P], we[:, :], start=False)
                i.then_inc(gate0_ps.sem, 1)

            def pos(ph):
                t = ph.a
                u = claim(ph, "pos")
                cs_up.wait(pe, t)
                mm(u[:, 0, 0:NC * E0], upper[:, :], oh[:, :, :].rearrange("p c e -> p (c e)"), stop=False)
                mm(u[:, 0, 0:NC * E0], ones[:, :], cs[:, :, :].rearrange("p c e -> p (c e)"), start=False
                   ).then_inc(pos_ps.sem, 1)

            def v1(ph):
                u = claim(ph, "v1")
                h32_up.wait(pe, ph.a, 2)
                for c in range(NC):
                    i = mm(u[:, 0, c * P:(c + 1) * P], h32[:, c * P:(c + 1) * P], wv[:, :])
                i.then_inc(v1_ps.sem, 1)

            def tv_step(ph):
                u = claim(ph, "tv")
                vt_up.wait(pe, ph.a)
                for c in range(NC):
                    i = mm(u[:, 0, 0:D], ones[:, :], vt[:, c, :], start=c == 0, stop=c == NC - 1)
                i.then_inc(tv_ps.sem, 1)

            def proj1(ph, g):
                t = ph.a
                u = claim(ph, "proj1", g)
                hlo_up.wait(pe, t, 1)
                for k in range(2):
                    w_hi = w1[:, 0, k, g, :, :].rearrange("p a m -> p (a m)")
                    w_lo = w1[:, 1, k, g, :, :].rearrange("p a m -> p (a m)")
                    i = split3(u[0:96, k, :], w_hi, w_lo, hT[:, 0, :], hT[:, 1, :])
                i.then_inc(proj1_ps.sem, 1)

            def max1(ph, g, k):
                t, b = ph.a, g % 2
                u = claim(ph, "max1", g, k)
                h, half = k // 2, k % 2
                lo1_up.wait(pe, t, 2 * g)
                km_up.wait(pe, t, HG * g + h)
                for j in range(2):
                    c = 2 * half + j
                    i = mm(u[:, j, :], X1[b][0:96, c * P:(c + 1) * P], K1[b][0:96, h, :])
                i.then_inc(max1_ps.sem, 1)

            def mt1(ph, g):
                u = claim(ph, "mt1", g)
                max1_up.wait(pe, ph.a, 8 * g + 7)
                for c in range(NC):
                    i = pe.transpose(u[0:4, 0, c * P:(c + 1) * P], nm1[:, g % 2, c, :], ident[:, :])
                i.then_inc(mt1_ps.sem, 1)

            def sc1(ph, g, jc, hp):
                t, b = ph.a, g % 2
                u = claim(ph, "sc1", g, jc, hp)
                m1_up.wait(pe, t, g)
                for i2 in range(2):
                    i = mm(u[:, i2, :], K1[b][:, 2 * hp + i2, jc * P:(jc + 1) * P], X1[b][:, :])
                i.then_inc(sc1_ps.sem, 1)

            def pv1(ph, g, jc):
                t, n = ph.a, 2 * (NC * g + jc)
                p1_up.wait(pe, t, n + 1)
                if g == 0 and jc == 0:
                    ones1_up.wait(pe, t)
                    v1_up.wait(pe, t)
                if g and jc == 0:
                    ot1_up.wait(pe, t, 2 * g - 2)
                for h in range(HG):
                    i = mm(O[QR * h:QR * h + QR, :], V1[:, jc, HG * g + h, :], Pt[:, (n + h // 2) % 4, h % 2, :],
                           start=jc == 0, stop=jc == NC - 1)
                i.then_inc(pv1_ps.sem, 1)

            def d1(ph, g):
                t = ph.a
                u = claim(ph, "d1", g)
                if isinstance(t, int) and g == 0:
                    pe.wait_ge(s_tabx, 48)
                for h in range(HG):
                    hh = HG * g + h
                    r = slice(QR * h, QR * h + QR)
                    mm(u[r, 0, 0:2 * P], V1[:, 3, hh, :], biasd[:, hh, :], stop=False)
                    i = mm(u[r, 0, P:2 * P], V1[:, 2, hh, :], biasd[:, hh, 0:P], start=False)
                i.then_inc(d1_ps.sem, 1)

            def nat(ph, g):
                t = ph.a
                u = claim(ph, "nat", g)
                ot1_up.wait(pe, t, 2 * g + 1)
                for c in range(6):
                    i = pe.transpose(u[:, c // NC, (c % NC) * P:(c % NC + 1) * P],
                                     OT[g % 2][:, c * P:(c + 1) * P], ident[:, :])
                i.then_inc(nat_ps.sem, 1)

            def route(ph):
                t = ph.a
                u = claim(ph, "route")
                h32_up.wait(pe, t, 3)
                for c in range(NC):
                    i = mm(u[:, 0, 16 * c:16 * c + 16], h32[:, c * P:(c + 1) * P],
                           wr[:, :, :].rearrange("p k e -> p (k e)"))
                i.then_inc(route_ps.sem, 1)

            def gu(ph, n):
                f = ph.f
                u = claim(ph, "gu", n)
                if n == 0:
                    hlo_up.wait(pe, f, 2)
                i2, c0 = (n // 2) % 2, 128 * (n % 2)
                ws_up.wait(pe, f, 2 * (n // 2) + 1)
                for k in range(2):
                    i = split3(u[:, k, :], ws[:, i2, 0, k, c0:c0 + P], ws[:, i2, 1, k, c0:c0 + P],
                               fT[:, 0, :], fT[:, 1, :])
                i.then_inc(gu_ps.sem, 1)

            def down(ph, n):
                f, e, fc = ph.f, n // FC, n % FC
                hs_up.wait(pe, f, n)
                if fc == 0 and e:
                    acc_up.wait(pe, f, e - 1)
                for c in range(NC):
                    i = mm(Y[:, c, :], hs[:, n % 4, c * P:(c + 1) * P], wd[:, e, fc, :],
                           start=fc == 0 and c == 0, stop=fc == FC - 1 and c == NC - 1, skip_group_check=True)
                i.then_inc(down_ps.sem, 1)

            run(pe, {"gates": gates_step, "ht": ht, "v0": v0, "proj0": proj0, "max0": max0, "mt0": mt0,
                     "sc0": sc0, "pv0": pv0, "z0": z0, "out0": out0, "gate0": gate0, "pos": pos, "v1": v1,
                     "tv": tv_step, "proj1": proj1, "max1": max1, "mt1": mt1, "sc1": sc1, "pv1": pv1,
                     "d1": d1, "nat": nat, "route": route, "gu": gu, "down": down})


def kernel(L0_attn_x, L0_attn_Wq, L0_attn_Wk, L0_attn_Wv, L0_attn_Wout, L0_attn_bout, L0_ffn_w_gate,
           L0_ffn_w_expert, L0_ffn_b_expert, L0_c, L0_wmod, L1_attn_Wq, L1_attn_Wk, L1_attn_Wv,
           L1_attn_bias_table, L1_attn_ln_gamma, L1_attn_ln_beta, L1_ffn_w_router, L1_ffn_w_gating,
           L1_ffn_w_gate, L1_ffn_w_up, L1_ffn_w_down, L1_c, L1_wmod):
    import concourse.bacc as bacc
    from concourse.bass_utils import run_bass_kernel_spmd

    def a(v):
        return np.ascontiguousarray(v)

    wmod = np.stack([np.asarray(L0_wmod).reshape(D, 6, D), np.asarray(L1_wmod).reshape(D, 6, D)], axis=1)
    table = np.asarray(L1_attn_bias_table)
    arrays = {
        "x": a(L0_attn_x),
        "cT": a(np.stack([np.asarray(L0_c).T, np.asarray(L1_c).T], axis=1)),
        "wmod": a(wmod),
        "wqkv0": a(np.concatenate([L0_attn_Wq, L0_attn_Wk, L0_attn_Wv], axis=1)),
        "wout0": a(L0_attn_Wout),
        "bout0": a(L0_attn_bout),
        "wg0": a(L0_ffn_w_gate),
        "we0": a(L0_ffn_w_expert),
        "be0": a(np.asarray(L0_ffn_b_expert).reshape(1, D)),
        "wqk1": a(np.stack([np.asarray(L1_attn_Wq).T, np.asarray(L1_attn_Wk).T], axis=1)),
        "wv1T": a(np.asarray(L1_attn_Wv).T),
        "table": a(table[::-1].T),
        "t_last": a(table[-1]),
        "gamma": a(L1_attn_ln_gamma),
        "beta": a(L1_attn_ln_beta),
        "wr1": a(np.stack([L1_ffn_w_router, L1_ffn_w_gating], axis=1)),
        "wgu1": a(np.stack([np.asarray(L1_ffn_w_gate), np.asarray(L1_ffn_w_up)], axis=0).transpose(2, 1, 0, 3)),
        "wd1": a(np.asarray(L1_ffn_w_down).reshape(E1, FC, P, D).transpose(2, 0, 1, 3)),
    }
    nc = bacc.Bacc("TRN2", target_bir_lowering=False, num_devices=1)
    args = [nc.dram_tensor(n, v.shape, mybir.dt.from_np(v.dtype), kind="ExternalInput").ap()
            for n, v in arrays.items()]
    out = nc.dram_tensor("out", (B, S, D), F32, kind="ExternalOutput").ap()
    build_program(nc, *args, out)
    return run_bass_kernel_spmd(nc, [arrays], core_ids=[0]).results[0]["out"]
```

```python
import numpy as np
import concourse.bass as bass
from concourse import mybir
from concourse.alu_op_type import AluOpType as ALU
from contextlib import ExitStack

F32 = mybir.dt.float32
F32R = mybir.dt.float32r
I32 = mybir.dt.int32
ACT = mybir.ActivationFunctionType
X = mybir.AxisListType.X

B, S, D = 16, 512, 128
P = 128
NC = S // P
EPS = 1e-5
H0, DH0 = 8, 64
PAIRS = H0 // 2
E0, CAP = 8, 100
SCALE0 = DH0 ** -0.5
H1 = 16
DH1 = D // H1
G, HG = 4, 4
QR = HG * DH1
SCALE1 = D ** -0.5
TAB = 255
E1, FF = 8, 512
FC = FF // P
TEMP = 0.1
NH = 3
NU = 3
NF = E1 * FC


def attention0_steps():
    steps = [("proj0", 0), ("v0", 0), ("v0", 1)] + [("max0", 0, k) for k in range(4)]
    steps += [("proj0", 1), ("mt0", 0)]
    for p in range(PAIRS):
        more = p + 1 < PAIRS
        for jc in range(NC):
            steps.append(("sc0", p, jc))
            if jc:
                steps.append(("pv0", p, jc - 1))
            if jc == 1 and p:
                steps.append(("z0", p - 1))
                if not more:
                    steps += [("rz0", p - 1, q) for q in range(4)]
            if jc == 2 and not more:
                steps += [("gates",), ("xp",)]
            for k in ((), (0, 1), (2,), (3,))[jc] if more else ():
                steps.append(("max0", p + 1, k))
                if k and p:
                    steps.append(("rz0", p - 1, k - 1))
        if more:
            steps.append(("mt0", p + 1))
        if p + 2 < PAIRS:
            steps.append(("proj0", p + 2))
        if more and p:
            steps.append(("rz0", p - 1, 3))
        steps.append(("pv0", p, NC - 1))
    return steps + [("z0", PAIRS - 1)] + [("rz0", PAIRS - 1, q) for q in range(4)]


def attention1_steps():
    steps = [("proj1", 0)] + [("max1", 0, k) for k in (0, 1)] + [("v1",)]
    steps += [("max1", 0, k) for k in (2, 3, 4)] + [("proj1", 1)]
    steps += [("max1", 0, k) for k in (5, 6, 7)] + [("tv",), ("mt1", 0)]
    for g in range(G):
        for jc in range(NC):
            steps.append(("sc1", g, jc, 0))
            if g + 1 < G:
                steps.append(("max1", g + 1, 2 * jc))
            if jc and g < G - 1:
                steps.append(("pv1", g, jc - 1))
            steps.append(("sc1", g, jc, 1))
            if jc and g == G - 1:
                steps.append(("pv1", g, jc - 1))
            if g + 1 < G:
                steps.append(("max1", g + 1, 2 * jc + 1))
            if jc == 1 and 0 < g < G - 1:
                steps.append(("nat", g - 1))
        if g + 2 < G:
            steps.append(("proj1", g + 2))
        steps.append(("pv1", g, NC - 1))
        if g + 1 < G:
            steps.append(("mt1", g + 1))
        if g == G - 1:
            steps.append(("nat", g - 1))
        steps.append(("d1", g))
    return steps + [("nat", G - 1)]


def mixture_steps():
    steps = []
    for n in range(NF + 2):
        if n < NF:
            steps.append(("gu", n))
        if n >= 2:
            steps.append(("down", n - 2))
    return steps


ATTENTION1 = attention1_steps()
CUT = ATTENTION1.index(("sc1", G - 1, 0, 1)) + 1
A_STEPS = ([("load",), ("mod",), ("ln", 0), ("lnb", 0), ("ht", 0), ("sel",)] + attention0_steps()
           + [("out0",), ("ln", 1), ("lnb", 1), ("ht", 1), ("gate0",), ("pos",),
              ("ln", 2), ("lnb", 2), ("ht", 2)]
           + ATTENTION1[:CUT])
NORMS = [("post1",), ("norm1",), ("ln", 4), ("lnb", 4), ("ht", 3), ("route",)]
F_STEPS = [("keep",)] + ATTENTION1[CUT:] + NORMS + mixture_steps()
AFTER = {("load",): [("keep",)], ("lnb", 0): ATTENTION1[CUT:-4], ("ht", 0): ATTENTION1[-4:],
         ("max0", 0, 3): [("post1",)], ("mt0", 0): [("norm1",)], ("sc0", 0, 0): [("ln", 4)],
         ("sc0", 0, 1): [("lnb", 4)], ("pv0", 0, 1): [("ht", 3)], ("sc0", 0, 3): [("route",)]}
CHUNKS = {("pv0", 1, 1): 1, ("pv0", 2, 1): 1, ("pv0", 2, 2): 1, ("pv0", 3, 0): 1, ("pv0", 3, 1): 1,
          ("pv0", 3, 2): 1, ("pv0", 3, 3): 2, ("z0", 3): 1, ("out0",): 1, ("ln", 1): 1, ("lnb", 1): 1,
          ("ht", 1): 1, ("gate0",): 1, ("pos",): 1, ("ln", 2): 1, ("lnb", 2): 1, ("ht", 2): 1,
          ("proj1", 0): 1, ("mt1", 0): 1}
CHUNKS.update({("max0", p, 3): 1 for p in range(1, PAIRS)})
CHUNKS.update({("max1", g, k): 1 for g in range(1, G) for k in (1, 3, 5)})


def loop_steps():
    steps, rest = [], mixture_steps()
    for s in A_STEPS:
        steps.append(s)
        steps += AFTER.get(s, [])
        for _ in range(CHUNKS.get(s, 0)):
            steps.append(rest.pop(0))
            if rest[0][0] == "down":
                steps.append(rest.pop(0))
        if s == ("max1", G - 1, 7):
            steps += rest
    assert not [s for s in rest if s[0] == "gu"]
    return steps


LOOP_STEPS = loop_steps()
F_SET = set(F_STEPS)
assert len(LOOP_STEPS) == len(A_STEPS) + len(F_STEPS)
UNITS = {"gates", "ht", "v0", "proj0", "max0", "mt0", "sc0", "z0", "out0", "gate0", "pos", "v1", "tv",
         "proj1", "max1", "mt1", "sc1", "d1", "nat", "route", "gu"}


class Phase:

    def __init__(self, steps, a, f):
        self.steps, self.a, self.f = steps, a, f
        using = [s for s in steps if s[0] in UNITS]
        first = -len(using) % NU
        self.slot, self.before, last = {}, {}, [None] * NU
        for n, s in enumerate(using):
            u = (first + n) % NU
            self.slot[s], self.before[s], last[u] = u, last[u], s
        self.last = last

    def of(self, *s):
        return self.f if s in F_SET else self.a


class Signal:

    def __init__(self, sem, per, base=0):
        self.sem, self.per, self.base = sem, per, base

    def wait(self, eng, batch, n=0):
        assert -self.per <= n < self.per
        if isinstance(batch, int) and batch * self.per + n + 1 <= 0:
            return
        eng.wait_ge(self.sem, batch * self.per + (n + 1 + self.base))


class Chain:

    def __init__(self, sem, per):
        self.sem, self.per, self.n = sem, per, 0

    def start(self):
        self.n = 0

    def link(self, ins):
        self.n += 1
        ins.then_inc(self.sem, 1)

    def wait(self, eng, batch):
        eng.wait_ge(self.sem, batch * self.per + self.n)

    def end(self):
        assert self.n == self.per, (self.sem, self.n)


def build_program(nc, x, cT, wmod, wqkv0, wout0, bout0, wg0, we0, be0, wqk1, wv1T, table, t_last,
                  gamma, beta, wr1, wgu1, wd1, out):
    ctx = ExitStack()
    with ctx:
        def sb(name, shape, dt=F32):
            return ctx.enter_context(nc.sbuf_tensor(name, shape, dt))

        def sem(name):
            return ctx.enter_context(nc.semaphore(name))

        def signal(name, per, base=0):
            return Signal(sem(name), per, base)

        w0 = sb("w0", [P, 2, 3 * H0 * DH0], F32R)
        wo = sb("wo", [P, PAIRS, D])
        bo = sb("bo", [P, D])
        wg = sb("wg", [P, E0])
        we = sb("we", [P, D])
        be = sb("be", [1, D])
        w1 = sb("w1", [P, 2, 2, G, 3, QR], F32R)
        wv = sb("wv", [P, D])
        biasd = sb("biasd", [P, H1, 2 * P])
        tlast = sb("tlast", [P, H1])
        t254 = sb("t254", [P, H1, DH1])
        wr = sb("wr", [P, 2, E1])
        wgu = sb("wgu", [P, E1, 2, FF])
        wd = sb("wd", [P, E1, FC, D])
        wgate = sb("wgate", [P, 2, 2, D])
        ident = sb("ident", [P, P])
        upper = sb("upper", [P, P])
        ones = sb("ones", [P, P])
        rev = sb("rev", [P, E0])
        mask = sb("mask", [96, HG])
        neghalf = sb("neghalf", [P, NC])
        sT = sb("sT", [P, 2, B])
        modc = sb("modc", [P, 8, B])
        gam = sb("gam", [P, D])
        bet = sb("bet", [P, D])
        xin = sb("xin", [P, NC, D])
        modb = sb("modb", [P, 8])
        modf = sb("modf", [P, 2])
        gates = sb("gates", [P, 4, D])
        st = sb("st", [P, NC, 6])
        mv = sb("mv", [P, NC, 2])
        ve = sb("ve", [P, NC])
        idle = sb("idle", [1, 2])
        rstd = sb("rstd", [P, NC])
        nrm = sb("nrm", [P, NC, D])
        h32 = sb("h32", [P, S])
        hT = sb("hT", [P, 2, S], F32R)
        gbo = sb("gbo", [P, D])
        xres = sb("xres", [P, NC, D])
        qk = sb("qk", [P, 2, 4, 2, S], F32R)
        V = sb("V", [P, NC, H0 * DH0])
        Pt = sb("Pt", [P, NC, 2, S])
        PS = sb("PS", [P, 2, S])
        oT = sb("oT", [P, PAIRS, S])
        att = sb("att", [P, NC, D])
        nm0 = sb("nm0", [P, 2, NC, 2])
        nm1 = sb("nm1", [P, 2, NC, HG])
        sm = sb("sm", [P, NC, 2, E1])
        sm2 = sb("sm2", [P, NC, 2, E1])
        sm3 = sb("sm3", [P, NC, E1])
        sc4 = sb("sc4", [P, 8, NC])
        cs = sb("cs", [P, NC, E0])
        oh = sb("oh", [P, NC, E0])
        tv = sb("tv", [P, D])
        ks = sb("ks", [96, S], F32R)
        rz1 = sb("rz1", [P, NC, HG])
        g1 = sb("g1", [P, D])
        fT = sb("fT", [P, 2, S], F32R)
        xf = sb("xf", [P, NC, D])
        gbf = sb("gbf", [P, D])
        cw = sb("cw", [P, NC, E1])
        hs = sb("hs", [P, NH, S])
        th = sb("th", [P, 2, S])
        acc = sb("acc", [P, NC, D])
        ws = sb("ws", [P, 2, 2, 2, FF // 2], F32R)

        V1 = V[:, :, :].rearrange("p c (h m) -> p c h m", h=H1)
        X1 = [qk[:, i, 0, 0, :] for i in range(2)]
        K1 = [qk[:, i, 2:4, :, :].rearrange("p a b n -> p (a b) n") for i in range(2)]
        OT = [oT[:, 0:2, :].rearrange("p a n -> p (a n)")[:, 0:S + 2 * P],
              oT[:, 2:4, :].rearrange("p a n -> p (a n)")[:, 0:S + 2 * P]]
        scb = h32[:, 0:2 * P].rearrange("p (l m) -> p l m", l=2)
        rz0 = nrm[:, :, :].rearrange("p c d -> p (c d)")
        half = att
        vt = PS[:, 0, :].rearrange("p (c d) -> p c d", c=NC)
        fn = acc
        fh = hs[:, 0, :]
        stage = Pt[:, :, :, :].rearrange("p a b n -> p (a b n)")
        raw0 = stage[:, 0:1536]
        rawm = stage[:, 1536:2560].rearrange("p (a b) -> p a b", a=8)
        raw1 = stage[:, 2560:2816].rearrange("p (a b) -> p a b", a=2)
        rawt = stage[0:H1, 2816:3200]
        craw = stage[:, 3200:3200 + 2 * B].rearrange("p (a b) -> p a b", a=2)
        cth = stage[:, 3232:3232 + 2 * B].rearrange("p (a b) -> p a b", a=2)
        t0 = stage[0:H1, 3264:3265]
        tabx = nc.dram_tensor("tabx", (H1, 384), F32).ap()

        ring = [ctx.enter_context(nc.psum_tensor(f"ring{u}", [P, 2, S], F32)) for u in range(NU)]
        O = ctx.enter_context(nc.psum_tensor("O", [P, S], F32))
        Y = ctx.enter_context(nc.psum_tensor("Y", [P, NC, D], F32))

        s_wq = sem("loaded_w0")
        s_small = sem("loaded_small")
        s_w1 = sem("loaded_w1")
        s_mod = sem("loaded_mod")
        s_ffn = sem("loaded_ffn")
        s_tab = sem("loaded_table")
        s_tabx = sem("table_spread")
        s_const = sem("constants")
        s_gconst = sem("pool_constants")
        s_sel = sem("selector_rows")
        s_th = sem("tanh_c")
        s_silu = sem("silu_c")
        s_pm = sem("mod_products")
        s_modc = sem("mod_columns")
        s_wsp = sem("weights_split")
        s_init = sem("vector_init")
        gates_ps = signal("gates_ps", 1)
        ht_ps = signal("ht_ps", 3)
        htf_ps = signal("htf_ps", 1)
        v0_ps = signal("v0_ps", 2)
        proj0_ps = signal("proj0_ps", PAIRS)
        max0_ps = signal("max0_ps", 4 * PAIRS)
        mt0_ps = signal("mt0_ps", PAIRS)
        sc0_ps = signal("sc0_ps", NC * PAIRS)
        pv0_ps = signal("pv0_ps", NC * PAIRS)
        z0_ps = signal("z0_ps", PAIRS)
        out0_ps = signal("out0_ps", 1)
        gate0_ps = signal("gate0_ps", 1)
        pos_ps = signal("pos_ps", 1)
        v1_ps = signal("v1_ps", 1)
        tv_ps = signal("tv_ps", 1)
        proj1_ps = signal("proj1_ps", G)
        max1_ps = signal("max1_ps", 8 * G)
        mt1_ps = signal("mt1_ps", G)
        sc1_ps = signal("sc1_ps", 2 * NC * G)
        pv1_ps = signal("pv1_ps", NC * G)
        d1_ps = signal("d1_ps", G)
        nat_ps = signal("nat_ps", G)
        route_ps = signal("route_ps", 1)
        gu_ps = signal("gu_ps", NF)
        down_ps = signal("down_ps", NF)
        h32_up = signal("h32_up", 3)
        h32f_up = signal("h32f_up", 1)
        hhi_up = signal("hhi_up", 2)
        hhif_up = signal("hhif_up", 1)
        v0_up = signal("v0_up", 2)
        hi0_up = signal("hi0_up", 4 * PAIRS)
        m0_up = signal("m0_up", PAIRS)
        p0_up = signal("p0_up", NC * PAIRS)
        zc_up = signal("zc_up", PAIRS)
        oc0_up = signal("oc0_up", PAIRS)
        e0_up = signal("e0_up", 1)
        v1_up = signal("v1_up", 1)
        tv_up = signal("tv_up", 1)
        hi1_up = signal("hi1_up", 2 * G)
        m1_up = signal("m1_up", G)
        p1_up = signal("p1_up", 2 * NC * G)
        ot1_up = signal("ot1_up", 2 * G)
        er_up = signal("er_up", 2)
        wshi_up = signal("wshi_up", 2 * E1)
        th_up = signal("th_up", NF)
        gates_up = signal("gates_up", 1)
        ve_up = signal("ve_up", 3)
        vef_up = signal("vef_up", 2)
        nrm_up = signal("nrm_up", 3)
        nrmf_up = signal("nrmf_up", 2)
        hlo_up = signal("hlo_up", 2)
        hlof_up = signal("hlof_up", 1)
        lo0_up = signal("lo0_up", 4 * PAIRS)
        max0_up = signal("max0_up", 4 * PAIRS)
        rz0_up = signal("rz0_up", 4 * PAIRS)
        o0_up = signal("o0_up", PAIRS)
        ga0_up = signal("ga0_up", 1)
        d0_up = signal("d0_up", 1)
        cs_up = signal("cs_up", 1)
        kept_up = signal("kept_up", 1)
        y0_up = signal("y0_up", 1)
        lo1_up = signal("lo1_up", 2 * G)
        max1_up = signal("max1_up", 8 * G)
        att_up = signal("att_up", G)
        xf_up = signal("xf_up", 1)
        rt_up = signal("rt_up", 1)
        cw_up = signal("cw_up", 1)
        hs_up = signal("hs_up", NF)
        gs_up = signal("gs_up", NF)
        acc_up = signal("acc_up", E1)
        fout_up = signal("fout_up", 1, 1)
        dve_a = Chain(sem("vector_a"), 25)
        dve_f = Chain(sem("vector_f"), 20)
        sel_up = signal("sel_up", 2)
        modb_up = signal("modb_up", 2)
        xp_up = signal("xp_up", 1)
        rstd_up = signal("rstd_up", 3)
        rstdf_up = signal("rstdf_up", 2)
        ps0_up = signal("ps0_up", 3 * PAIRS)
        ones1_up = signal("ones1_up", 1)
        vt_up = signal("vt_up", 1)
        km_up = signal("km_up", HG * G)
        g1_up = signal("g1_up", 1)
        xb_up = signal("xb_up", 1)
        gbf_up = signal("gbf_up", 2)
        ws_up = signal("ws_up", 2 * E1)
        pool_a = Chain(sem("pool_a"), 2)
        hold_a = Chain(sem("pool_hold_a"), 9)
        hold_f = Chain(sem("pool_hold_f"), 1)
        x_in = signal("x_in", 16)
        dup0 = [[signal(f"dup0_{i}{h}", 32 * PAIRS // 2) for h in range(2)] for i in range(2)]
        stored = signal("stored", 16, 16)

        def freed_by(s):
            k = s[0]
            if k == "gates":
                return gates_up, 0
            if k == "ht":
                return {0: (hhi_up, 0), 1: (h32_up, 1), 2: (hhi_up, 1), 3: (hhif_up, 0)}[s[1]]
            if k == "v0":
                return v0_up, s[1]
            if k == "proj0":
                return lo0_up, 4 * s[1] + 3
            if k == "max0":
                return max0_up, 4 * s[1] + s[2]
            if k == "mt0":
                return m0_up, s[1]
            if k == "sc0":
                return p0_up, NC * s[1] + s[2]
            if k == "z0":
                return zc_up, s[1]
            if k == "out0":
                return ga0_up, 0
            if k == "gate0":
                return y0_up, 0
            if k == "pos":
                return kept_up, 0
            if k == "v1":
                return v1_up, 0
            if k == "tv":
                return tv_up, 0
            if k == "proj1":
                return lo1_up, 2 * s[1] + 1
            if k == "max1":
                return max1_up, 8 * s[1] + s[2]
            if k == "mt1":
                return m1_up, s[1]
            if k == "sc1":
                return p1_up, 2 * (NC * s[1] + s[2]) + s[3]
            if k == "d1":
                return ot1_up, 2 * s[1] + 1
            if k == "nat":
                return att_up, s[1]
            if k == "route":
                return rt_up, 0
            return gs_up, s[1]

        first = Phase(A_STEPS, 0, None)
        last = Phase(F_STEPS, None, B - 1)

        def run(eng, parts, chains=()):
            def walk(phase):
                for c in chains:
                    c.start()
                for s in phase.steps:
                    if s[0] in parts:
                        parts[s[0]](phase, *s[1:])

            walk(first)
            with eng.Fori(1, B) as t:
                walk(Phase(LOOP_STEPS, t, t - 1))
            walk(last)

        def unit(ph, *s):
            return ring[ph.slot[s]]

        def pieces(n):
            return [n + 2] if n and n % 2 == 0 and n + 2 < NF else []

        def as32(ap):
            return ap.bitcast(F32)

        block = ctx.enter_context(nc.Block())

        @block.sync
        def _(sp):
            xv = x.rearrange("b (c p) d -> b p c d", p=P)
            ov = out.rearrange("b (c p) d -> b p c d", p=P)
            sp.dma_start(xin[:, :, :], xv[0]).then_inc(x_in.sem, 16)
            sp.dma_start(craw, cT).then_inc(s_mod, 16)
            sp.dma_start(rawm.rearrange("p (l k) d -> p l k d", l=2)[:, :, 0:2, :],
                         wmod[:, :, 0:2, :]).then_inc(s_mod, 16)
            sp.dma_start(rawm.rearrange("p (l k) d -> p l k d", l=2)[:, :, 2:4, :],
                         wmod[:, :, 3:5, :]).then_inc(s_mod, 16)
            for k in range(2):
                sp.dma_start(wgate[:, :, k, :], wmod[:, :, 2 + 3 * k, :]).then_inc(s_mod, 16)
            sp.dma_start(raw0, wqkv0).then_inc(s_wq, 16)
            for dst, src in ((wo[:, :, :], wout0.rearrange("(a p) d -> p a d", p=P)),
                             (bo[:, :], bout0.partition_broadcast(P)), (wg[:, :], wg0), (we[:, :], we0),
                             (be[:, :], be0), (gam[:, :], gamma.partition_broadcast(P)),
                             (bet[:, :], beta.partition_broadcast(P)),
                             (tlast[:, :], t_last.partition_broadcast(P)), (wv[:, :], wv1T),
                             (wr[:, :, :], wr1)):
                sp.dma_start(dst, src).then_inc(s_small, 16)
            sp.dma_start(raw1, wqk1).then_inc(s_w1, 16)
            sp.wait_ge(s_tab, 1)
            sp.dma_start(rawt[:, P:P + TAB], table).then_inc(s_tabx, 16)
            sp.dma_start(wgu[:, :, :, :], wgu1).then_inc(s_ffn, 16)
            sp.dma_start(wd[:, :, :, :], wd1).then_inc(s_ffn, 16)
            sp.wait_ge(s_tab, 2)
            sp.dma_start(tabx, rawt).then_inc(stored.sem, 16)
            sp.wait_ge(stored.sem, 16)
            sp.dma_start(biasd[:, :, :], bass.AP(tensor=tabx.tensor, offset=0,
                                                 ap=[[1, P], [384, H1], [1, 2 * P]])).then_inc(s_tabx, 16)

            def load(ph):
                t = ph.a
                if isinstance(t, int):
                    return
                nrm_up.wait(sp, t, -3)
                xp_up.wait(sp, t, -1)
                sp.dma_start(xin[:, :, :], xv[t]).then_inc(x_in.sem, 16)

            def proj0(ph, p):
                t, i = ph.a, p % 2
                for h in range(2):
                    r, o = (slice(0, 64), slice(64, 128)) if h == 0 else (slice(64, 128), slice(0, 64))
                    hi0_up.wait(sp, t, 4 * p + h)
                    sp.dma_start(as32(qk[0:64, i, 2, h, :]), as32(qk[r, i, 0, h, :])
                                 ).then_inc(dup0[i][h].sem, 16)
                    hi0_up.wait(sp, t, 4 * p + 2 + h)
                    sp.dma_start(as32(qk[o, i, 1, h, :]), as32(qk[r, i, 1, h, :])
                                 ).then_inc(dup0[i][h].sem, 16)

            def down(ph, n):
                if n == NF - 1:
                    fout_up.wait(sp, ph.f, 0)
                    sp.dma_start(ov[ph.f], acc[:, :, :]).then_inc(stored.sem, 16)

            run(sp, {"load": load, "proj0": proj0, "down": down})
            sp.wait_ge(stored.sem, 16 * (B + 1))

        @block.gpsimd
        def _(pool):
            pool.memset(ident[:, :], 0.0).then_inc(s_gconst, 1)
            pool.memset(upper[:, :], 1.0).then_inc(s_gconst, 1)
            pool.memset(mask[:, :], 1.0).then_inc(s_gconst, 1)
            pool.wait_ge(s_gconst, 3)
            pool.affine_select(out=ident[:, :], in_=ident[:, :], compare_op=ALU.not_equal, fill=1.0,
                               base=0, pattern=[[-1, P]], channel_multiplier=1).then_inc(s_gconst, 1)
            pool.affine_select(out=upper[:, :], in_=upper[:, :], compare_op=ALU.is_ge, fill=0.0,
                               base=0, pattern=[[1, P]], channel_multiplier=-1).then_inc(s_gconst, 1)
            for qd in range(3):
                for lo in (True, False):
                    mk = mask[QR * qd:QR * qd + QR, :]
                    pool.affine_select(out=mk, in_=mk, compare_op=ALU.is_ge, fill=0.0,
                                       base=0 if lo else DH1 - 1, pattern=[[-DH1 if lo else DH1, HG]],
                                       channel_multiplier=1 if lo else -1).then_inc(s_gconst, 1)
                    pool.wait_ge(s_gconst, 6 + 2 * qd + (not lo))
            pool.memset(neghalf[:, :], -0.5).then_inc(s_gconst, 1)
            for e in range(E0):
                pool.memset(rev[:, e:e + 1], float(E0 - e)).then_inc(s_gconst, 1)
            pool.memset(cs[:, 0, :], 0.0).then_inc(s_gconst, 1)
            pool.memset(rawt, 0.0).then_inc(s_tab, 1)

            def hold(chain, batch):
                if chain.n or (chain is hold_a and not isinstance(batch, int)):
                    chain.wait(pool, batch)
                k = int(chain is hold_f)
                chain.link(pool.tensor_tensor(idle[0:1, k:k + 1], neghalf[0:1, 0:1], neghalf[0:1, 0:1],
                                              ALU.mult))

            def keep(ph):
                fout_up.wait(pool, ph.f, -1)
                hold(hold_f, ph.f)
                pool.tensor_copy(gbf[:, :], gates[:, 3, :]).then_inc(gbf_up.sem, 1)
                pool.tensor_copy(modf[:, :], modb[:, 6:8]).then_inc(gbf_up.sem, 1)

            def mod(ph):
                t = ph.a
                if isinstance(t, int):
                    pool.wait_ge(s_modc, 2)
                gates_ps.wait(pool, t, -1)
                hhi_up.wait(pool, t, -1)
                gbf_up.wait(pool, t, -1)
                hold(hold_a, ph.a)
                pool.tensor_copy(modb[:, :].unsqueeze(2), modc[:, :, bass.ds(t, 1)]).then_inc(modb_up.sem, 1)

            def sel(ph):
                for i in range(2):
                    sc1_ps.wait(pool, ph.a, -9 if i == 0 else -1)
                    hold(hold_a, ph.a)
                    pool.tensor_copy(qk[0:96, i, 3, :, :], ident[0:96, 64:66].unsqueeze(2)
                                     .broadcast_to([96, 2, S])).then_inc(sel_up.sem, 1)

            def gates_step(ph):
                t = ph.a
                hlo_up.wait(pool, t, 0)
                hold(hold_a, ph.a)
                pool.tensor_copy(scb, sT[:, :, bass.ds(t, 1)].broadcast_to([P, 2, P])).then_inc(modb_up.sem, 1)

            def xp(ph):
                t = ph.a
                gates_up.wait(pool, t, 0)
                xf_up.wait(pool, t, -1)
                x_in.wait(pool, t, 15)
                if isinstance(t, int):
                    pool.wait_ge(s_small, 160)
                pool.tensor_tensor(gbo[:, :], gates[:, 0, :], bo[:, :], ALU.mult).then_inc(pool_a.sem, 1)
                pool_a.n += 1
                pool_a.wait(pool, t)
                pool.tensor_tensor(xres[:, :, :], xin[:, :, :], gbo[:, :].unsqueeze(1).broadcast_to([P, NC, D]),
                                   ALU.add).then_inc(xp_up.sem, 1)

            def ln(ph, n):
                sig, up, batch = (ve_up, rstd_up, ph.a) if n < 3 else (vef_up, rstdf_up, ph.f)
                sig.wait(pool, batch, n % 3)
                pool.tensor_tensor(rstd[:, :], ve[:, :], neghalf[:, :], ALU.pow).then_inc(up.sem, 1)

            def pv0(ph, p, jc):
                t = ph.a
                if jc == 0:
                    return
                p0_up.wait(pool, t, NC * p + jc)
                if jc == 1:
                    if p:
                        z0_ps.wait(pool, t, p - 1)
                    pool.tensor_tensor(PS[:, :, :], Pt[:, 0, :, :], Pt[:, 1, :, :], ALU.add
                                       ).then_inc(ps0_up.sem, 1)
                else:
                    ps0_up.wait(pool, t, 3 * p + jc - 2)
                    pool.tensor_tensor(PS[:, :, :], PS[:, :, :], Pt[:, jc, :, :], ALU.add
                                       ).then_inc(ps0_up.sem, 1)

            def out0(ph):
                out0_ps.wait(pool, ph.a)
                hold(hold_a, ph.a)
                pool.memset(V1[:, :, :, DH1:], 1.0).then_inc(ones1_up.sem, 1)

            def v1(ph):
                t = ph.a
                v1_up.wait(pool, t)
                pool.tensor_tensor(vt.rearrange("p c (h m) -> p c h m", h=H1), V1[:, :, :, 0:DH1],
                                   t254[:, :, :].unsqueeze(1).broadcast_to([P, NC, H1, DH1]),
                                   ALU.mult).then_inc(vt_up.sem, 1)

            def tv_step(ph):
                t = ph.a
                pool.tensor_tensor(g1[:, :], gates[:, 2, :], gam[:, :], ALU.mult).then_inc(g1_up.sem, 1)
                pool.tensor_tensor(gbo[:, :], gates[:, 2, :], bet[:, :], ALU.mult).then_inc(pool_a.sem, 1)
                pool_a.n += 1
                pool_a.wait(pool, t)
                nrm_up.wait(pool, t, 2)
                pool.tensor_tensor(xres[:, :, :], xres[:, :, :],
                                   gbo[:, :].unsqueeze(1).broadcast_to([P, NC, D]), ALU.add
                                   ).then_inc(xb_up.sem, 1)

            def proj1(ph, g):
                t = ph.a
                lo1_up.wait(pool, t, 2 * g + 1)
                hold(hold_a, ph.a)
                for h in range(HG):
                    pool.tensor_scalar(K1[g % 2][0:96, h, :], as32(ks[:, :]), mask[:, h:h + 1], 1.0,
                                       ALU.mult, ALU.mult).then_inc(km_up.sem, 1)

            def post1(ph):
                ln(ph, 3)

            def gu(ph, n):
                gs_up.wait(pool, ph.f, n)
                pool.tensor_tensor(hs[:, n % NH, :], hs[:, n % NH, :], th[:, n % 2, :], ALU.mult
                                   ).then_inc(hs_up.sem, 1)
                for m in pieces(n):
                    lo_parts(ph.f, m)

            def lo_parts(f, m):
                e, q, i = m // 4, (m // 2) % 2, (m // 2) % 2
                wshi_up.wait(pool, f, m // 2)
                pool.tensor_tensor(ws[:, i, 1, :, :], wgu[:, e, :, q * 256:(q + 1) * 256],
                                   as32(ws[:, i, 0, :, :]), ALU.subtract).then_inc(ws_up.sem, 1)

            def norm1(ph):
                for m in (0, 2):
                    lo_parts(ph.f, m)

            pool.wait_ge(s_gconst, 21)
            for i in range(2):
                pool.wait_ge(s_sel, i + 1)
                pool.tensor_copy(K1[i][96:128, :, :],
                                 ident[96:128, 96:96 + HG].unsqueeze(2).broadcast_to([32, HG, S])
                                 ).then_inc(s_gconst, 1)
            pool.wait_ge(s_gconst, 23)
            run(pool, {"keep": keep, "mod": mod, "sel": sel, "gates": gates_step, "xp": xp, "ln": ln,
                    "pv0": pv0, "out0": out0, "v1": v1,
                       "tv": tv_step, "proj1": proj1, "post1": post1, "norm1": norm1, "gu": gu},
                [pool_a, hold_a, hold_f])

        @block.scalar
        def _(act):
            ID, EXP, TANH, COPY = ACT.Identity, ACT.Exp, ACT.Tanh, ACT.Copy
            act.wait_ge(s_mod, 80)
            act.activation(cth, craw, TANH, scale=0.5).then_inc(s_th, 1)

            def ht(ph, l):
                t = ph.a
                u = unit(ph, "ht", l)
                if l == 3:
                    htf_ps.wait(act, ph.f)
                    gbf_up.wait(act, ph.f, 1)
                    s, c = modf[:, 0:1], modf[:, 1:2]
                    act.activation(fh, u[:, 0, :], ID, bias=s, scale=c).then_inc(h32f_up.sem, 1)
                    act.activation(fT[:, 0, :], u[:, 0, :], ID, bias=s, scale=c).then_inc(hhif_up.sem, 1)
                    return
                ht_ps.wait(act, t, l)
                if l == 0:
                    modb_up.wait(act, t, 0)
                k = 2 * l
                s, c = modb[:, k:k + 1], modb[:, k + 1:k + 2]
                act.activation(h32[:, :], u[:, 0, :], ID, bias=s, scale=c).then_inc(h32_up.sem, 1)
                if l != 1:
                    act.activation(hT[:, 0, :], u[:, 0, :], ID, bias=s, scale=c).then_inc(hhi_up.sem, 1)

            def v0(ph, i):
                v0_ps.wait(act, ph.a, i)
                d1_ps.wait(act, ph.a, -1)
                pv1_ps.wait(act, ph.a, -1)
                act.activation(V[:, 2 * i:2 * i + 2, :], unit(ph, "v0", i)[:, :, :], COPY).then_inc(v0_up.sem, 1)

            def proj0(ph, p):
                proj0_ps.wait(act, ph.a, p)
                u, i = unit(ph, "proj0", p), p % 2
                for k in range(2):
                    for h in range(2):
                        r = slice(64 * h, 64 * h + 64)
                        act.activation(qk[r, i, k, h, :], u[r, k, :], COPY).then_inc(hi0_up.sem, 1)

            def mt0(ph, p):
                mt0_ps.wait(act, ph.a, p)
                u = unit(ph, "mt0", p)
                act.activation(qk[64:66, p % 2, 2, :, :], u[0:2, 0, :].unsqueeze(1).broadcast_to([2, 2, S]),
                               COPY).then_inc(m0_up.sem, 1)

            def sc0(ph, p, jc):
                t = ph.a
                sc0_ps.wait(act, t, NC * p + jc)
                if p == 0:
                    pv1_ps.wait(act, t, -1)
                else:
                    pv0_ps.wait(act, t, NC * (p - 1) + jc)
                    ps0_up.wait(act, t, 3 * (p - 1) + max(jc - 1, 0))
                act.activation(Pt[:, jc, :, :], unit(ph, "sc0", p, jc)[:, :, :], EXP,
                               scale=SCALE0).then_inc(p0_up.sem, 1)

            def pv0(ph, p, jc):
                if jc < NC - 1:
                    return
                pv0_ps.wait(act, ph.a, NC * p + NC - 1)
                nat_ps.wait(act, ph.a, -1)
                act.activation(oT[:, p, :], O[:, :], COPY).then_inc(oc0_up.sem, 1)

            def z0(ph, p):
                z0_ps.wait(act, ph.a, p)
                if p:
                    o0_up.wait(act, ph.a, p - 1)
                act.activation(rz0, unit(ph, "z0", p)[:, 0, :], COPY).then_inc(zc_up.sem, 1)

            def gate0(ph):
                d0_up.wait(act, ph.a)
                act.activation(sm2[:, :, 0, :], sm[:, :, 0, :], EXP).then_inc(e0_up.sem, 1)

            def v1(ph):
                v1_ps.wait(act, ph.a)
                u = unit(ph, "v1")
                act.activation(V1[:, :, :, 0:DH1], u[:, 0, :].rearrange("p (c h m) -> p c h m", c=NC, h=H1),
                               COPY).then_inc(v1_up.sem, 1)

            def tv_step(ph):
                tv_ps.wait(act, ph.a)
                act.activation(tv[:, :], unit(ph, "tv")[:, 0, 0:D], COPY).then_inc(tv_up.sem, 1)

            def proj1(ph, g):
                t = ph.a
                proj1_ps.wait(act, t, g)
                u = unit(ph, "proj1", g)
                act.activation(X1[g % 2][0:96, :], u[0:96, 0, :], COPY).then_inc(hi1_up.sem, 1)
                if g:
                    km_up.wait(act, t, HG * g - 1)
                act.activation(ks[:, :], u[0:96, 1, :], COPY).then_inc(hi1_up.sem, 1)

            def mt1(ph, g):
                mt1_ps.wait(act, ph.a, g)
                act.activation(X1[g % 2][96:100, :], unit(ph, "mt1", g)[0:4, 0, :], COPY).then_inc(m1_up.sem, 1)

            def sc1(ph, g, jc, hp):
                t, n = ph.of("sc1", g, jc, hp), 2 * (NC * g + jc) + hp
                sc1_ps.wait(act, t, n)
                if n >= 4:
                    pv1_ps.wait(act, t, (n - 4) // 2)
                act.activation(Pt[:, n % 4, :, :], unit(ph, "sc1", g, jc, hp)[:, :, :], EXP,
                               scale=SCALE1).then_inc(p1_up.sem, 1)

            def d1(ph, g):
                t = ph.of("d1", g)
                pv1_ps.wait(act, t, NC * g + NC - 1)
                act.activation(OT[g % 2][:, 0:S], O[:, :], COPY).then_inc(ot1_up.sem, 1)
                d1_ps.wait(act, t, g)
                act.activation(OT[g % 2][:, S:S + 2 * P], unit(ph, "d1", g)[:, 0, 2 * P - 1::-1], COPY).then_inc(ot1_up.sem, 1)

            def norm1(ph):
                act.wait_ge(s_ffn, 32)
                for m in (0, 2):
                    hi_parts(ph.f, m)

            def route(ph):
                rt_up.wait(act, ph.f)
                act.activation(sm2[:, :, 0, :], sm[:, :, 0, :], EXP).then_inc(er_up.sem, 1)
                act.activation(sm2[:, :, 1, :], sm[:, :, 1, :], EXP, scale=1.0 / TEMP).then_inc(er_up.sem, 1)

            def gu(ph, n):
                f = ph.f
                gu_ps.wait(act, f, n)
                if n == 0:
                    route_ps.wait(act, f)
                if n >= NH:
                    down_ps.wait(act, f, n - NH)
                act.activation(hs[:, n % NH, :], unit(ph, "gu", n)[:, 1, :], COPY, scale=0.5)
                if n >= 2:
                    hs_up.wait(act, f, n - 2)
                act.activation(th[:, n % 2, :], unit(ph, "gu", n)[:, 0, :], TANH, scale=0.5).then_inc(th_up.sem, 1)
                for m in pieces(n):
                    hi_parts(f, m)

            def hi_parts(f, m):
                e, q, i = m // 4, (m // 2) % 2, (m // 2) % 2
                if m >= 4:
                    gu_ps.wait(act, f, m - 3)
                    ws_up.wait(act, f, m // 2 - 1)
                act.activation(ws[:, i, 0, :, :], wgu[:, e, :, q * 256:(q + 1) * 256], COPY
                               ).then_inc(wshi_up.sem, 1)

            run(act, {"norm1": norm1, "ht": ht, "v0": v0, "proj0": proj0, "mt0": mt0, "sc0": sc0,
                    "pv0": pv0, "z0": z0, "gate0": gate0, "v1": v1,
                      "tv": tv_step, "proj1": proj1, "mt1": mt1, "sc1": sc1, "d1": d1, "route": route, "gu": gu})

        @block.vector
        def _(dve):
            dve.memset(ones[:, :], 1.0).then_inc(s_const, 1)
            dve.memset(acc[:, :, :], 0.0).then_inc(fout_up.sem, 1)
            for i in range(2):
                dve.memset(as32(qk[:, i, :, :, :]), 0.0).then_inc(s_sel, 1)
            dve.wait_ge(s_th, 1)
            dve.scalar_tensor_tensor(cth, cth, 1.0, craw, ALU.add, ALU.mult).then_inc(s_silu, 1)
            dve.wait_ge(s_silu, 1)
            dve.tensor_scalar(sT[:, :, :], cth, 0.5, None, ALU.mult).then_inc(s_silu, 1)
            dve.wait_ge(s_wq, 16)
            dve.tensor_copy(w0[:, 0, :], raw0).then_inc(s_wsp, 1)
            dve.wait_ge(s_wsp, 1)
            dve.tensor_tensor(w0[:, 1, :], raw0, as32(w0[:, 0, :]), ALU.subtract).then_inc(s_wsp, 1)
            dve.wait_ge(s_w1, 16)
            for k in range(2):
                r = raw1[:, k, :].rearrange("p (g m) -> p g m", g=G).unsqueeze(2).broadcast_to([P, G, 3, QR])
                dve.tensor_copy(w1[:, 0, k, :, :, :], r).then_inc(s_wsp, 1)
                dve.wait_ge(s_wsp, 3 + 2 * k)
                dve.tensor_tensor(w1[:, 1, k, :, :, :], r, as32(w1[:, 0, k, :, :, :]), ALU.subtract
                                  ).then_inc(s_wsp, 1)
            dve.wait_ge(s_pm, 1)
            mp = ring[0][:, 0, 0:8 * B].rearrange("p (k b) -> p k b", k=8)
            dve.tensor_copy(modc[:, 0::2, :], mp[:, 0::2, :]).then_inc(s_modc, 1)
            dve.tensor_scalar(modc[:, 1::2, :], mp[:, 1::2, :], 1.0, None, ALU.add).then_inc(s_modc, 1)
            dve.wait_ge(s_tabx, 16)
            dve.tensor_copy(t0, rawt[:, P:P + 1]).then_inc(s_init, 1)
            dve.wait_ge(s_init, 1)
            dve.tensor_scalar(rawt[:, P:P + TAB], rawt[:, P:P + TAB], t0, None, ALU.subtract).then_inc(s_tab, 1)
            dve.wait_ge(s_small, 160)
            dve.tensor_copy(t254[:, :, :], tlast[:, :].unsqueeze(2).broadcast_to([P, H1, DH1])).then_inc(s_init, 1)

            A = dve_a

            def gates_step(ph):
                t = ph.a
                gates_ps.wait(dve, t)
                xb_up.wait(dve, t, -1)
                gbf_up.wait(dve, t, -1)
                gp = unit(ph, "gates")[:, 0, :].rearrange("p (k d) -> p k d", k=4)
                A.link(dve.tensor_scalar(half[:, :, :], gp, 0.0, 0.5, ALU.is_ge, ALU.subtract))
                A.wait(dve, t)
                A.link(dve.scalar_tensor_tensor(gates[:, :, :], half[:, :, :], 4.0, gp, ALU.mult, ALU.mult))
                A.wait(dve, t)
                dve.scalar_tensor_tensor(gates[:, :, :], gates[:, :, :], 0.5, half[:, :, :], ALU.max,
                                         ALU.mult).then_inc(gates_up.sem, 1)

            def ln(ph, n):
                if n < 3:
                    t, A, up = ph.a, dve_a, ve_up
                else:
                    t, A, up = ph.f, dve_f, vef_up
                if n == 0:
                    x_in.wait(dve, t, 15)
                src = (xin, xres, xres, att, xf)[n]
                for c in range(NC):
                    i = dve.bn_stats(st[:, c, :], src[:, c, :])
                A.link(i)
                A.wait(dve, t)
                dve.tensor_copy(ve[0:1, 0:1], st[0:1, 0, 0:1])
                for c in range(NC):
                    i = dve.bn_aggr(mv[:, c, :], st[:, c, :])
                A.link(i)
                A.wait(dve, t)
                dve.tensor_scalar(ve[:, :], mv[:, :, 1], EPS, None, ALU.add).then_inc(up.sem, 1)

            def lnb(ph, n):
                src, to = (xin, xres, xres, att, xf)[n], nrm if n < 3 else fn
                t, back, done = (ph.a, rstd_up, nrm_up) if n < 3 else (ph.f, rstdf_up, nrmf_up)
                back.wait(dve, t, n % 3)
                for c in range(NC):
                    i = dve.tensor_scalar(to[:, c, :], src[:, c, :], mv[:, c, 0:1], rstd[:, c:c + 1],
                                          ALU.subtract, ALU.mult)
                i.then_inc(done.sem, 1)

            def ht(ph, l):
                t = ph.a
                if l == 1:
                    return
                if l == 3:
                    hhif_up.wait(dve, ph.f)
                    dve.tensor_tensor(fT[:, 1, :], fh, as32(fT[:, 0, :]), ALU.subtract).then_inc(hlof_up.sem, 1)
                    return
                hhi_up.wait(dve, t, l // 2)
                dve.tensor_tensor(hT[:, 1, :], h32[:, :], as32(hT[:, 0, :]), ALU.subtract
                                  ).then_inc(hlo_up.sem, 1)

            def proj0(ph, p):
                t, i = ph.a, p % 2
                u = unit(ph, "proj0", p)
                for h in range(2):
                    r, o = (slice(0, 64), slice(64, 128)) if h == 0 else (slice(64, 128), slice(0, 64))
                    hi0_up.wait(dve, t, 4 * p + h)
                    dve.tensor_tensor(qk[o, i, 0, h, :], u[r, 0, :], as32(qk[r, i, 0, h, :]), ALU.subtract
                                      ).then_inc(lo0_up.sem, 1)
                for h in range(2):
                    r = slice(64 * h, 64 * h + 64)
                    hi0_up.wait(dve, t, 4 * p + 2 + h)
                    if p < 2 and h == 0:
                        sel_up.wait(dve, t, p)
                    dve.tensor_tensor(qk[0:64, i, 3, h, :], u[r, 1, :], as32(qk[r, i, 1, h, :]), ALU.subtract
                                      ).then_inc(lo0_up.sem, 1)

            def max0(ph, p, k):
                t = ph.a
                h, half = k // 2, k % 2
                max0_ps.wait(dve, t, 4 * p + k)
                dve.tensor_reduce(nm0[:, p % 2, 2 * half:2 * half + 2, h], unit(ph, "max0", p, k)[:, :, :], X,
                                  ALU.max, negate=True).then_inc(max0_up.sem, 1)

            def rz0_step(ph, p, q):
                t = ph.a
                zc_up.wait(dve, t, p)
                dve.reciprocal(rz0[:, q * P:(q + 1) * P], rz0[:, q * P:(q + 1) * P]).then_inc(rz0_up.sem, 1)
                if q == 3:
                    rz0_up.wait(dve, t, 4 * p + 3)
                    oc0_up.wait(dve, t, p)
                    dve.tensor_tensor(oT[:, p, :], oT[:, p, :], rz0, ALU.mult).then_inc(o0_up.sem, 1)

            def wide(g):
                return g.unsqueeze(1).broadcast_to([P, NC, D])

            def out0(ph):
                t = ph.a
                out0_ps.wait(dve, t)
                gates_up.wait(dve, t)
                y = unit(ph, "out0")[:, 0, :].rearrange("p (c d) -> p c d", c=NC)
                dve.tensor_tensor(nrm[:, :, :], y, wide(gates[:, 0, :]), ALU.mult).then_inc(ga0_up.sem, 1)
                ga0_up.wait(dve, t)
                xp_up.wait(dve, t)
                A.link(dve.tensor_tensor(xres[:, :, :], xres[:, :, :], nrm[:, :, :], ALU.add))
                A.wait(dve, t)

            def w8(ap):
                return ap.unsqueeze(2).broadcast_to([P, NC, E0])

            def gate0(ph):
                t = ph.a
                gate0_ps.wait(dve, t)
                lg = unit(ph, "gate0")[:, 0, 0:NC * E0].rearrange("p (c e) -> p c e", c=NC)
                A.link(dve.tensor_reduce(sc4[:, 0, :], lg, X, ALU.max))
                A.wait(dve, t)
                dve.tensor_tensor(sm[:, :, 0, :], lg, w8(sc4[:, 0, :]), ALU.subtract).then_inc(d0_up.sem, 1)
                d0_up.wait(dve, t)
                A.link(dve.scalar_tensor_tensor(sm3[:, :, :], sm[:, :, 0, :], 0.0,
                                                rev[:, :].unsqueeze(1).broadcast_to([P, NC, E0]),
                                                ALU.is_equal, ALU.mult))
                A.wait(dve, t)
                A.link(dve.tensor_reduce(sc4[:, 1, :], sm3[:, :, :], X, ALU.max))
                A.wait(dve, t)
                A.link(dve.tensor_tensor(oh[:, :, :], sm3[:, :, :], w8(sc4[:, 1, :]), ALU.is_equal))
                A.wait(dve, t)
                for c in range(1, NC):
                    i = dve.tensor_tensor(cs[:, c, :], cs[:, c - 1, :], oh[:, c - 1, :], ALU.add)
                    if c < NC - 1:
                        A.link(i)
                        A.wait(dve, t)
                i.then_inc(cs_up.sem, 1)
                y = unit(ph, "gate0")[:, 1, :].rearrange("p (c d) -> p c d", c=NC)
                dve.tensor_tensor(nrm[:, :, :], y, wide(gates[:, 1, :]), ALU.mult).then_inc(y0_up.sem, 1)
                e0_up.wait(dve, t)
                A.link(dve.tensor_reduce(sc4[:, 2, :], sm2[:, :, 0, :], X, ALU.add))
                A.wait(dve, t)
                A.link(dve.reciprocal(sc4[:, 3, :], sc4[:, 2, :]))

            def pos(ph):
                t = ph.a
                pos_ps.wait(dve, t)
                ps = unit(ph, "pos")[:, 0, 0:NC * E0].rearrange("p (c e) -> p c e", c=NC)
                dve.scalar_tensor_tensor(sm3[:, :, :], ps, float(CAP), oh[:, :, :], ALU.is_le, ALU.mult
                                         ).then_inc(kept_up.sem, 1)
                A.link(dve.tensor_tensor(cs[:, 0, :], cs[:, NC - 1, :], oh[:, NC - 1, :], ALU.add))
                kept_up.wait(dve, t)
                A.link(dve.tensor_reduce(sc4[:, 4, :], sm3[:, :, :], X, ALU.add))
                A.wait(dve, t)
                A.link(dve.tensor_tensor(sc4[:, 5, :], sc4[:, 4, :], sc4[:, 3, :], ALU.mult))
                A.wait(dve, t)
                y0_up.wait(dve, t)
                for c in range(NC):
                    i = dve.scalar_tensor_tensor(xres[:, c, :], nrm[:, c, :], sc4[:, 5, c:c + 1], xres[:, c, :],
                                                 ALU.mult, ALU.add)
                A.link(i)
                A.wait(dve, t)

            def proj1(ph, g):
                t = ph.a
                u = unit(ph, "proj1", g)
                hi1_up.wait(dve, t, 2 * g)
                dve.tensor_tensor(X1[g % 2][32:64, :], u[32:64, 0, :], as32(X1[g % 2][32:64, :]), ALU.subtract
                                  ).then_inc(lo1_up.sem, 1)
                hi1_up.wait(dve, t, 2 * g + 1)
                dve.tensor_tensor(ks[64:96, :], u[64:96, 1, :], as32(ks[64:96, :]), ALU.subtract
                                  ).then_inc(lo1_up.sem, 1)

            def max1(ph, g, k):
                t = ph.a
                h, half = k // 2, k % 2
                max1_ps.wait(dve, t, 8 * g + k)
                dve.tensor_reduce(nm1[:, g % 2, 2 * half:2 * half + 2, h], unit(ph, "max1", g, k)[:, :, :], X,
                                  ALU.max, negate=True).then_inc(max1_up.sem, 1)

            def nat(ph, g):
                t = ph.of("nat", g)
                C = dve_f if ("nat", g) in F_SET else dve_a
                nat_ps.wait(dve, t, g)
                u = unit(ph, "nat", g)
                o = u[:, 0, :].rearrange("p (c q m) -> p c q m", c=NC, q=HG)
                d = u[:, 1, 0:2 * P].rearrange("p (c q m) -> p c q m", c=2, q=HG)
                a = att[:, :, QR * g:QR * g + QR].rearrange("p c (q m) -> p c q m", q=HG)
                C.link(dve.reciprocal(rz1[:, :, :], o[:, :, :, DH1]))
                C.wait(dve, t)
                C.link(dve.tensor_tensor(a, o[:, :, :, 0:DH1],
                                         rz1[:, :, :].unsqueeze(3).broadcast_to([P, NC, HG, DH1]), ALU.mult))
                C.wait(dve, t)
                dve.tensor_tensor(a[:, 0:2], a[:, 0:2], d[:, :, :, 0:DH1], ALU.add).then_inc(att_up.sem, 1)
                if g == G - 3:
                    C.end()

            def post1(ph):
                f = ph.f
                tv_up.wait(dve, f)
                att_up.wait(dve, f, G - 1)
                dve_f.link(dve.tensor_tensor(att[:, :, :], att[:, :, :], wide(tv[:, :]), ALU.add))
                dve_f.wait(dve, f)
                ln(ph, 3)

            def norm1(ph):
                f, A = ph.f, dve_f
                stored.wait(dve, f, -1)
                lnb(ph, 3)
                nrmf_up.wait(dve, f, 0)
                g1_up.wait(dve, f)
                A.link(dve.tensor_tensor(fn[:, :, :], fn[:, :, :], wide(g1[:, :]), ALU.mult))
                A.wait(dve, f)
                xb_up.wait(dve, f)
                dve.tensor_tensor(xf[:, :, :], fn[:, :, :], xres[:, :, :], ALU.add).then_inc(xf_up.sem, 1)
                xf_up.wait(dve, f)

            def route(ph):
                t, A = ph.f, dve_f
                route_ps.wait(dve, t)
                lg = unit(ph, "route")[:, 0, 0:NC * 2 * E1].rearrange("p (c k e) -> p (c k) e", c=NC, k=2)
                d = sm[:, :, :, :].rearrange("p c k e -> p (c k) e")
                A.link(dve.tensor_reduce(sc4[:, 0:2, :].rearrange("p a c -> p (a c)"), lg, X, ALU.max))
                A.wait(dve, t)
                dve.tensor_tensor(d, lg, sc4[:, 0:2, :].rearrange("p a c -> p (a c)").unsqueeze(2)
                                  .broadcast_to([P, 2 * NC, E1]), ALU.subtract).then_inc(rt_up.sem, 1)
                er_up.wait(dve, t, 1)
                s2 = sc4[:, 2:4, :].rearrange("p a c -> p (a c)")
                A.link(dve.tensor_reduce(s2, sm2[:, :, :, :].rearrange("p c k e -> p (c k) e"), X, ALU.add))
                A.link(dve.tensor_tensor(sm3[:, :, :], sm2[:, :, 0, :], sm2[:, :, 1, :], ALU.mult))
                A.wait(dve, t)
                A.link(dve.reciprocal(s2, s2))
                A.wait(dve, t)
                s2v = s2.rearrange("p (c k) -> p c k", k=2)
                A.link(dve.tensor_tensor(sc4[:, 4, :], s2v[:, :, 0], s2v[:, :, 1], ALU.mult))
                A.wait(dve, t)
                A.link(dve.tensor_tensor(sm3[:, :, :], sm3[:, :, :], w8(sc4[:, 4, :]), ALU.mult))
                A.wait(dve, t)
                A.link(dve.tensor_reduce(sc4[:, 5, :], sm3[:, :, :], X, ALU.add))
                A.wait(dve, t)
                A.link(dve.tensor_scalar(sc4[:, 5, :], sc4[:, 5, :], 1e-9, None, ALU.add))
                A.wait(dve, t)
                A.link(dve.reciprocal(sc4[:, 6, :], sc4[:, 5, :]))
                A.wait(dve, t)
                dve.tensor_tensor(cw[:, :, :], sm3[:, :, :], w8(sc4[:, 6, :]), ALU.mult).then_inc(cw_up.sem, 1)

            def gu(ph, n):
                f = ph.f
                th_up.wait(dve, f, n)
                dve.scalar_tensor_tensor(th[:, n % 2, :], th[:, n % 2, :], 1.0, unit(ph, "gu", n)[:, 0, :],
                                         ALU.add, ALU.mult).then_inc(gs_up.sem, 1)

            def down(ph, n):
                f, e = ph.f, n // FC
                if n % FC != FC - 1:
                    return
                down_ps.wait(dve, f, n)
                if e == 0:
                    cw_up.wait(dve, f)
                    gbf_up.wait(dve, f, 1)
                else:
                    acc_up.wait(dve, f, e - 1)
                for c in range(NC):
                    if e == 0:
                        i = dve.tensor_scalar(acc[:, c, :], Y[:, c, :], cw[:, c, e:e + 1], None, ALU.mult)
                    else:
                        i = dve.scalar_tensor_tensor(acc[:, c, :], Y[:, c, :], cw[:, c, e:e + 1], acc[:, c, :],
                                                     ALU.mult, ALU.add)
                i.then_inc(acc_up.sem, 1)
                if e == E1 - 1:
                    acc_up.wait(dve, f, e)
                    dve_f.link(dve.tensor_tensor(acc[:, :, :], acc[:, :, :], wide(gbf[:, :]), ALU.mult))
                    dve_f.wait(dve, f)
                    dve.tensor_tensor(acc[:, :, :], acc[:, :, :], xf[:, :, :], ALU.add).then_inc(fout_up.sem, 1)
                    dve_f.end()

            run(dve, {"gates": gates_step, "ln": ln, "lnb": lnb, "norm1": norm1, "ht": ht, "proj0": proj0,
                    "max0": max0, "rz0": rz0_step,
                      "out0": out0, "gate0": gate0, "pos": pos, "proj1": proj1, "max1": max1, "nat": nat,
                      "post1": post1, "route": route, "gu": gu, "down": down}, [dve_a, dve_f])

        @block.tensor
        def _(pe):
            def mm(o, lhsT, rhs, start=True, stop=True, **k):
                return pe.matmul(o, lhsT, rhs, start=start, stop=stop, **k)

            pe.wait_ge(s_silu, 2)
            pe.wait_ge(s_mod, 80)
            mp = ring[0][:, 0, 0:8 * B].rearrange("p (k b) -> p k b", k=8)
            for k in range(8):
                i = mm(mp[:, k, :], rawm[:, k, :], sT[:, k // 4, :])
            i.then_inc(s_pm, 1)
            pe.wait_ge(s_modc, 2)
            pe.wait_ge(s_gconst, 23)
            pe.wait_ge(s_const, 1)
            pe.wait_ge(s_small, 160)
            pe.wait_ge(s_wsp, 6)

            def claim(ph, *s):
                prev = ph.before[s]
                if prev is not None:
                    sig, n = freed_by(prev)
                    sig.wait(pe, ph.of(*prev), n)
                elif ph is not first:
                    sig, n = freed_by(first.last[ph.slot[s]])
                    if ph.a is None:
                        sig.wait(pe, B - 1, n)
                    else:
                        sig.wait(pe, ph.a, n - sig.per)
                return ring[ph.slot[s]]

            def split3(o, w_hi, w_lo, m_hi, m_lo):
                mm(o, w_hi, m_hi, stop=False)
                mm(o, w_lo, m_hi, start=False, stop=False)
                return mm(o, w_hi, m_lo, start=False)

            def gates_step(ph):
                t = ph.a
                u = claim(ph, "gates")
                modb_up.wait(pe, t, 1)
                for l in range(2):
                    i = mm(u[:, 0, 256 * l:256 * l + 256], scb[:, l, :],
                           wgate[:, l, :, :].rearrange("p k d -> p (k d)"))
                i.then_inc(gates_ps.sem, 1)

            def ht(ph, l):
                u = claim(ph, "ht", l)
                if l < 3:
                    nrm_up.wait(pe, ph.a, l)
                else:
                    nrmf_up.wait(pe, ph.f, 1)
                src, up = (nrm, ht_ps) if l < 3 else (fn, htf_ps)
                for c in range(NC):
                    i = pe.transpose(u[:, 0, c * P:(c + 1) * P], src[:, c, :], ident[:, :])
                i.then_inc(up.sem, 1)

            def v0(ph, i2):
                t = ph.a
                u = claim(ph, "v0", i2)
                hlo_up.wait(pe, t, 0)
                for k in range(2):
                    c = 2 * i2 + k
                    hi, lo = hT[:, 0, c * P:(c + 1) * P], hT[:, 1, c * P:(c + 1) * P]
                    i = split3(u[:, k, :], hi, lo, w0[:, 0, 1024:], w0[:, 1, 1024:])
                i.then_inc(v0_ps.sem, 1)

            def proj0(ph, p):
                t = ph.a
                u = claim(ph, "proj0", p)
                hlo_up.wait(pe, t, 0)
                for k in range(2):
                    cols = slice(512 * k + 128 * p, 512 * k + 128 * p + 128)
                    i = split3(u[:, k, :], w0[:, 0, cols], w0[:, 1, cols], hT[:, 0, :], hT[:, 1, :])
                i.then_inc(proj0_ps.sem, 1)

            def max0(ph, p, k):
                t, b = ph.a, p % 2
                u = claim(ph, "max0", p, k)
                h, half = k // 2, k % 2
                lo0_up.wait(pe, t, 4 * p + h)
                dup0[b][h].wait(pe, t, 32 * (p // 2) + 31)
                for j in range(2):
                    c = 2 * half + j
                    i = mm(u[:, j, :], qk[:, b, 0, h, c * P:(c + 1) * P], qk[:, b, 1, h, :])
                i.then_inc(max0_ps.sem, 1)

            def mt0(ph, p):
                u = claim(ph, "mt0", p)
                max0_up.wait(pe, ph.a, 4 * p + 3)
                for c in range(NC):
                    i = pe.transpose(u[0:2, 0, c * P:(c + 1) * P], nm0[:, p % 2, c, :], ident[:, :])
                i.then_inc(mt0_ps.sem, 1)

            def sc0(ph, p, jc):
                t, b = ph.a, p % 2
                u = claim(ph, "sc0", p, jc)
                m0_up.wait(pe, t, p)
                lo0_up.wait(pe, t, 4 * p + 3)
                if p < 2 and jc == 0:
                    sel_up.wait(pe, t, p)
                for h in range(2):
                    c = slice(jc * P, (jc + 1) * P)
                    mm(u[:, h, :], qk[:, b, 1, h, c], qk[:, b, 0, h, :], stop=False)
                    i = mm(u[:, h, :], qk[0:96, b, 3, h, c], qk[0:96, b, 2, h, :], start=False)
                i.then_inc(sc0_ps.sem, 1)

            def pv0(ph, p, jc):
                t = ph.a
                p0_up.wait(pe, t, NC * p + jc)
                if p == 0:
                    v0_up.wait(pe, t, jc // 2)
                    if jc == 0:
                        ot1_up.wait(pe, t, -2)
                if jc == 0 and p:
                    oc0_up.wait(pe, t, p - 1)
                for h in range(2):
                    i = mm(O[64 * h:64 * h + 64, :], V[:, jc, 128 * p + 64 * h:128 * p + 64 * h + 64],
                           Pt[:, jc, h, :], start=jc == 0, stop=jc == NC - 1)
                i.then_inc(pv0_ps.sem, 1)

            def z0(ph, p):
                t = ph.a
                u = claim(ph, "z0", p)
                ps0_up.wait(pe, t, 3 * p + 2)
                for h in range(2):
                    i = mm(u[64 * h:64 * h + 64, 0, :], ones[:, 0:64], PS[:, h, :])
                i.then_inc(z0_ps.sem, 1)

            def out0(ph):
                t = ph.a
                u = claim(ph, "out0")
                for p in range(PAIRS):
                    o0_up.wait(pe, t, p)
                    for c in range(NC):
                        i = mm(u[:, 0, c * P:(c + 1) * P], oT[:, p, c * P:(c + 1) * P], wo[:, p, :],
                               start=p == 0 and c == 0, stop=p == PAIRS - 1 and c == NC - 1,
                               skip_group_check=True)
                i.then_inc(out0_ps.sem, 1)

            def gate0(ph):
                t = ph.a
                u = claim(ph, "gate0")
                h32_up.wait(pe, t, 1)
                for c in range(NC):
                    mm(u[:, 0, c * E0:(c + 1) * E0], h32[:, c * P:(c + 1) * P], wg[:, :])
                for c in range(NC):
                    mm(u[:, 1, c * P:(c + 1) * P], ones[0:1, :], be[0:1, :], stop=False)
                    i = mm(u[:, 1, c * P:(c + 1) * P], h32[:, c * P:(c + 1) * P], we[:, :], start=False)
                i.then_inc(gate0_ps.sem, 1)

            def pos(ph):
                t = ph.a
                u = claim(ph, "pos")
                cs_up.wait(pe, t)
                mm(u[:, 0, 0:NC * E0], upper[:, :], oh[:, :, :].rearrange("p c e -> p (c e)"), stop=False)
                mm(u[:, 0, 0:NC * E0], ones[:, :], cs[:, :, :].rearrange("p c e -> p (c e)"), start=False
                   ).then_inc(pos_ps.sem, 1)

            def v1(ph):
                u = claim(ph, "v1")
                h32_up.wait(pe, ph.a, 2)
                for c in range(NC):
                    i = mm(u[:, 0, c * P:(c + 1) * P], h32[:, c * P:(c + 1) * P], wv[:, :])
                i.then_inc(v1_ps.sem, 1)

            def tv_step(ph):
                u = claim(ph, "tv")
                vt_up.wait(pe, ph.a)
                for c in range(NC):
                    i = mm(u[:, 0, 0:D], ones[:, :], vt[:, c, :], start=c == 0, stop=c == NC - 1)
                i.then_inc(tv_ps.sem, 1)

            def proj1(ph, g):
                t = ph.a
                u = claim(ph, "proj1", g)
                hlo_up.wait(pe, t, 1)
                for k in range(2):
                    w_hi = w1[:, 0, k, g, :, :].rearrange("p a m -> p (a m)")
                    w_lo = w1[:, 1, k, g, :, :].rearrange("p a m -> p (a m)")
                    i = split3(u[0:96, k, :], w_hi, w_lo, hT[:, 0, :], hT[:, 1, :])
                i.then_inc(proj1_ps.sem, 1)

            def max1(ph, g, k):
                t, b = ph.a, g % 2
                u = claim(ph, "max1", g, k)
                h, half = k // 2, k % 2
                lo1_up.wait(pe, t, 2 * g)
                km_up.wait(pe, t, HG * g + h)
                for j in range(2):
                    c = 2 * half + j
                    i = mm(u[:, j, :], X1[b][0:96, c * P:(c + 1) * P], K1[b][0:96, h, :])
                i.then_inc(max1_ps.sem, 1)

            def mt1(ph, g):
                u = claim(ph, "mt1", g)
                max1_up.wait(pe, ph.a, 8 * g + 7)
                for c in range(NC):
                    i = pe.transpose(u[0:4, 0, c * P:(c + 1) * P], nm1[:, g % 2, c, :], ident[:, :])
                i.then_inc(mt1_ps.sem, 1)

            def sc1(ph, g, jc, hp):
                t, b = ph.of("sc1", g, jc, hp), g % 2
                u = claim(ph, "sc1", g, jc, hp)
                m1_up.wait(pe, t, g)
                for i2 in range(2):
                    i = mm(u[:, i2, :], K1[b][:, 2 * hp + i2, jc * P:(jc + 1) * P], X1[b][:, :])
                i.then_inc(sc1_ps.sem, 1)

            def pv1(ph, g, jc):
                t, n = ph.of("pv1", g, jc), 2 * (NC * g + jc)
                p1_up.wait(pe, t, n + 1)
                if g == 0 and jc == 0:
                    ones1_up.wait(pe, t)
                    v1_up.wait(pe, t)
                if g and jc == 0:
                    ot1_up.wait(pe, t, 2 * g - 2)
                for h in range(HG):
                    i = mm(O[QR * h:QR * h + QR, :], V1[:, jc, HG * g + h, :], Pt[:, (n + h // 2) % 4, h % 2, :],
                           start=jc == 0, stop=jc == NC - 1)
                i.then_inc(pv1_ps.sem, 1)

            def d1(ph, g):
                t = ph.of("d1", g)
                u = claim(ph, "d1", g)
                if isinstance(t, int) and g == 0:
                    pe.wait_ge(s_tabx, 32)
                for h in range(HG):
                    hh = HG * g + h
                    r = slice(QR * h, QR * h + QR)
                    mm(u[r, 0, 0:2 * P], V1[:, 3, hh, :], biasd[:, hh, :], stop=False)
                    i = mm(u[r, 0, P:2 * P], V1[:, 2, hh, :], biasd[:, hh, 0:P], start=False)
                i.then_inc(d1_ps.sem, 1)

            def nat(ph, g):
                t = ph.of("nat", g)
                u = claim(ph, "nat", g)
                ot1_up.wait(pe, t, 2 * g + 1)
                for c in range(6):
                    i = pe.transpose(u[:, c // NC, (c % NC) * P:(c % NC + 1) * P],
                                     OT[g % 2][:, c * P:(c + 1) * P], ident[:, :])
                i.then_inc(nat_ps.sem, 1)

            def route(ph):
                u = claim(ph, "route")
                h32f_up.wait(pe, ph.f)
                for c in range(NC):
                    i = mm(u[:, 0, 16 * c:16 * c + 16], fh[:, c * P:(c + 1) * P],
                           wr[:, :, :].rearrange("p k e -> p (k e)"))
                i.then_inc(route_ps.sem, 1)

            def gu(ph, n):
                f = ph.f
                u = claim(ph, "gu", n)
                if n == 0:
                    hlof_up.wait(pe, f)
                i2, c0 = (n // 2) % 2, 128 * (n % 2)
                ws_up.wait(pe, f, n // 2)
                for k in range(2):
                    i = split3(u[:, k, :], ws[:, i2, 0, k, c0:c0 + P], ws[:, i2, 1, k, c0:c0 + P],
                               fT[:, 0, :], fT[:, 1, :])
                i.then_inc(gu_ps.sem, 1)

            def down(ph, n):
                f, e, fc = ph.f, n // FC, n % FC
                hs_up.wait(pe, f, n)
                if fc == 0 and e:
                    acc_up.wait(pe, f, e - 1)
                for c in range(NC):
                    i = mm(Y[:, c, :], hs[:, n % NH, c * P:(c + 1) * P], wd[:, e, fc, :],
                           start=fc == 0 and c == 0, stop=fc == FC - 1 and c == NC - 1, skip_group_check=True)
                i.then_inc(down_ps.sem, 1)

            run(pe, {"gates": gates_step, "ht": ht, "v0": v0, "proj0": proj0, "max0": max0, "mt0": mt0,
                     "sc0": sc0, "pv0": pv0, "z0": z0, "out0": out0, "gate0": gate0, "pos": pos, "v1": v1,
                     "tv": tv_step, "proj1": proj1, "max1": max1, "mt1": mt1, "sc1": sc1, "pv1": pv1,
                     "d1": d1, "nat": nat, "route": route, "gu": gu, "down": down})


def kernel(L0_attn_x, L0_attn_Wq, L0_attn_Wk, L0_attn_Wv, L0_attn_Wout, L0_attn_bout, L0_ffn_w_gate,
           L0_ffn_w_expert, L0_ffn_b_expert, L0_c, L0_wmod, L1_attn_Wq, L1_attn_Wk, L1_attn_Wv,
           L1_attn_bias_table, L1_attn_ln_gamma, L1_attn_ln_beta, L1_ffn_w_router, L1_ffn_w_gating,
           L1_ffn_w_gate, L1_ffn_w_up, L1_ffn_w_down, L1_c, L1_wmod):
    import concourse.bacc as bacc
    from concourse.bass_utils import run_bass_kernel_spmd

    def a(v):
        return np.ascontiguousarray(v)

    wmod = np.stack([np.asarray(L0_wmod).reshape(D, 6, D), np.asarray(L1_wmod).reshape(D, 6, D)], axis=1)
    table = np.asarray(L1_attn_bias_table)
    arrays = {
        "x": a(L0_attn_x),
        "cT": a(np.stack([np.asarray(L0_c).T, np.asarray(L1_c).T], axis=1)),
        "wmod": a(wmod),
        "wqkv0": a(np.concatenate([L0_attn_Wq, L0_attn_Wk, L0_attn_Wv], axis=1)),
        "wout0": a(L0_attn_Wout),
        "bout0": a(L0_attn_bout),
        "wg0": a(L0_ffn_w_gate),
        "we0": a(L0_ffn_w_expert),
        "be0": a(np.asarray(L0_ffn_b_expert).reshape(1, D)),
        "wqk1": a(np.stack([np.asarray(L1_attn_Wq).T, np.asarray(L1_attn_Wk).T], axis=1)),
        "wv1T": a(np.asarray(L1_attn_Wv).T),
        "table": a(table[::-1].T),
        "t_last": a(table[-1]),
        "gamma": a(L1_attn_ln_gamma),
        "beta": a(L1_attn_ln_beta),
        "wr1": a(np.stack([L1_ffn_w_router, L1_ffn_w_gating], axis=1)),
        "wgu1": a(np.stack([np.asarray(L1_ffn_w_gate), np.asarray(L1_ffn_w_up)], axis=0).transpose(2, 1, 0, 3)),
        "wd1": a(np.asarray(L1_ffn_w_down).reshape(E1, FC, P, D).transpose(2, 0, 1, 3)),
    }
    nc = bacc.Bacc("TRN2", target_bir_lowering=False, num_devices=1)
    args = [nc.dram_tensor(n, v.shape, mybir.dt.from_np(v.dtype), kind="ExternalInput").ap()
            for n, v in arrays.items()]
    out = nc.dram_tensor("out", (B, S, D), F32, kind="ExternalOutput").ap()
    build_program(nc, *args, out)
    return run_bass_kernel_spmd(nc, [arrays], core_ids=[0]).results[0]["out"]
```
